# Optimizing a Trainium2 kernel written in Bass

```python
import numpy as np
import jax
import jax.numpy as jnp

def _softmax(x, axis=-1):
    return jax.nn.softmax(x, axis=axis)

def _gelu(x):
    return jax.nn.gelu(x, approximate=True)

def _silu(x):
    return jax.nn.silu(x)

def _sigmoid(x):
    return jax.nn.sigmoid(x)

def _layernorm(x, axis=-1, eps=1e-05):
    m = jnp.mean(x, axis=axis, keepdims=True)
    v = jnp.var(x, axis=axis, keepdims=True)
    return (x - m) / jnp.sqrt(v + eps)

def _scatter_add(tgt, idx, src, axis=0):
    return tgt.at[idx].add(src)

def _segment_sum(src, seg, n):
    return jax.ops.segment_sum(src, seg, n)
kernel_name = 'mk_seq_preln_d1_jaxref_r4_e9d2fe'

def setup_inputs(seed: int=0):
    np.random.seed(seed)
    _w = jnp.asarray

    def _L0_attn_setup():
        import jax, jax.numpy as jnp
        import numpy as np
        D_MODEL, D_STATE, D_CONV, EXPAND = (256, 16, 4, 2)
        D_INNER = EXPAND * D_MODEL
        B_SZ, L_SEQ = (2, 512)
        LN_EPS = 1e-05

        def _selective_scan(u, dt, A, Bp, Cp):

            def step(h, inp):
                dt_t, B_t, C_t, u_t = inp
                dA = jnp.exp(jnp.clip(dt_t[:, :, None] * A, -20.0, 0.0))
                dB_u = jnp.clip(dt_t[:, :, None] * B_t[:, None, :] * u_t[:, :, None], -10.0, 10.0)
                h = jnp.clip(h * dA + dB_u, -100.0, 100.0)
                y = jnp.einsum('bdn,bn->bd', h, C_t)
                return (h, y)
            h0 = jnp.zeros((u.shape[0], u.shape[2], A.shape[0]), dtype=u.dtype)
            xs = (jnp.swapaxes(dt, 0, 1), jnp.swapaxes(Bp, 0, 1), jnp.swapaxes(Cp, 0, 1), jnp.swapaxes(u, 0, 1))
            _, ys = jax.lax.scan(step, h0, xs)
            return jnp.swapaxes(ys, 0, 1)
        key = jax.random.key(seed)
        ks = jax.random.split(key, 8)
        x = jax.random.normal(ks[0], (B_SZ, L_SEQ, D_MODEL), dtype=jnp.float32)
        W_in = jax.random.normal(ks[1], (2 * D_INNER, D_MODEL), dtype=jnp.float32) * (1.0 / np.sqrt(D_MODEL))
        conv_w = jax.random.normal(ks[2], (D_INNER, 1, D_CONV), dtype=jnp.float32) * (1.0 / np.sqrt(D_CONV))
        conv_b = jax.random.normal(ks[3], (D_INNER,), dtype=jnp.float32) * 0.01
        W_x = jax.random.normal(ks[4], (2 * D_STATE + 1, D_INNER), dtype=jnp.float32) * (1.0 / np.sqrt(D_INNER))
        W_dt = jax.random.uniform(ks[5], (D_INNER, 1), dtype=jnp.float32, minval=-0.01, maxval=0.01)
        b_dt = jnp.full((D_INNER,), 0.1, dtype=jnp.float32)
        A_log = jnp.log(jnp.arange(1, D_STATE + 1, dtype=jnp.float32) * 0.1)
        D_param = jnp.ones((D_INNER,), dtype=jnp.float32)
        W_out = jax.random.normal(ks[6], (D_MODEL, D_INNER), dtype=jnp.float32) * (1.0 / np.sqrt(D_INNER))
        ln_g = jnp.ones((D_INNER,), dtype=jnp.float32)
        ln_b = jnp.zeros((D_INNER,), dtype=jnp.float32)
        return {'x': x, 'W_in': W_in, 'conv_w': conv_w, 'conv_b': conv_b, 'W_x': W_x, 'W_dt': W_dt, 'b_dt': b_dt, 'A_log': A_log, 'D_param': D_param, 'W_out': W_out, 'ln_g': ln_g, 'ln_b': ln_b}
    _L0_attn_in = _L0_attn_setup()

    def _L0_ffn_setup():
        import jax, jax.numpy as jnp
        import numpy as np
        DIM = 256

        def _reference_tuple_inner(x, W_r, W_k, W_v, mu_r, mu_k):
            B, T, C = x.shape
            x_prev = jnp.concatenate([jnp.zeros((B, 1, C), x.dtype), x[:, :-1, :]], axis=1)
            xr = mu_r * x + (1.0 - mu_r) * x_prev
            xk = mu_k * x + (1.0 - mu_k) * x_prev
            r = jax.nn.sigmoid(jnp.einsum('btc,dc->btd', xr, W_r))
            k = jnp.einsum('btc,dc->btd', xk, W_k)
            k_act = jnp.square(jax.nn.relu(k))
            out = r * jnp.einsum('btc,dc->btd', k_act, W_v)
            new_state = x[:, -1, :]
            return (out, new_state)
        key = jax.random.key(seed)
        ks = jax.random.split(key, 6)
        B, T, C = (8, 512, DIM)
        x = jax.random.normal(ks[0], (B, T, C), dtype=jnp.float32)
        s = 1.0 / np.sqrt(C)
        W_r = jax.random.uniform(ks[1], (C, C), jnp.float32, -s, s)
        W_k = jax.random.uniform(ks[2], (C, C), jnp.float32, -s, s)
        W_v = jax.random.uniform(ks[3], (C, C), jnp.float32, -s, s)
        mu_r = jax.random.uniform(ks[4], (C,), jnp.float32)
        mu_k = jax.random.uniform(ks[5], (C,), jnp.float32)
        return {'x': x, 'W_r': W_r, 'W_k': W_k, 'W_v': W_v, 'mu_r': mu_r, 'mu_k': mu_k}
    _L0_ffn_in = _L0_ffn_setup()
    _d = {'L0_attn_x': _L0_attn_in['x'], 'L0_attn_W_in': _L0_attn_in['W_in'], 'L0_attn_conv_w': _L0_attn_in['conv_w'], 'L0_attn_conv_b': _L0_attn_in['conv_b'], 'L0_attn_W_x': _L0_attn_in['W_x'], 'L0_attn_W_dt': _L0_attn_in['W_dt'], 'L0_attn_b_dt': _L0_attn_in['b_dt'], 'L0_attn_A_log': _L0_attn_in['A_log'], 'L0_attn_D_param': _L0_attn_in['D_param'], 'L0_attn_W_out': _L0_attn_in['W_out'], 'L0_attn_ln_g': _L0_attn_in['ln_g'], 'L0_attn_ln_b': _L0_attn_in['ln_b'], 'L0_ffn_W_r': _L0_ffn_in['W_r'], 'L0_ffn_W_k': _L0_ffn_in['W_k'], 'L0_ffn_W_v': _L0_ffn_in['W_v'], 'L0_ffn_mu_r': _L0_ffn_in['mu_r'], 'L0_ffn_mu_k': _L0_ffn_in['mu_k']}
    _x0 = _d['L0_attn_x']
    _d['L0_attn_x'] = jax.random.normal(jax.random.fold_in(jax.random.key(seed), 1), (16, 512, 256), dtype=_x0.dtype)
    del _x0
    return _d

def reference(L0_attn_x, L0_attn_W_in, L0_attn_conv_w, L0_attn_conv_b, L0_attn_W_x, L0_attn_W_dt, L0_attn_b_dt, L0_attn_A_log, L0_attn_D_param, L0_attn_W_out, L0_attn_ln_g, L0_attn_ln_b, L0_ffn_W_r, L0_ffn_W_k, L0_ffn_W_v, L0_ffn_mu_r, L0_ffn_mu_k):

    def _L0_attn_ref(x, W_in, conv_w, conv_b, W_x, W_dt, b_dt, A_log, D_param, W_out, ln_g, ln_b):
        import jax, jax.numpy as jnp
        import numpy as np
        D_MODEL, D_STATE, D_CONV, EXPAND = (256, 16, 4, 2)
        D_INNER = EXPAND * D_MODEL
        B_SZ, L_SEQ = (2, 512)
        LN_EPS = 1e-05

        def _selective_scan(u, dt, A, Bp, Cp):

            def step(h, inp):
                dt_t, B_t, C_t, u_t = inp
                dA = jnp.exp(jnp.clip(dt_t[:, :, None] * A, -20.0, 0.0))
                dB_u = jnp.clip(dt_t[:, :, None] * B_t[:, None, :] * u_t[:, :, None], -10.0, 10.0)
                h = jnp.clip(h * dA + dB_u, -100.0, 100.0)
                y = jnp.einsum('bdn,bn->bd', h, C_t)
                return (h, y)
            h0 = jnp.zeros((u.shape[0], u.shape[2], A.shape[0]), dtype=u.dtype)
            xs = (jnp.swapaxes(dt, 0, 1), jnp.swapaxes(Bp, 0, 1), jnp.swapaxes(Cp, 0, 1), jnp.swapaxes(u, 0, 1))
            _, ys = jax.lax.scan(step, h0, xs)
            return jnp.swapaxes(ys, 0, 1)
        B, L, _ = x.shape
        d_state = A_log.shape[0]
        d_inner = D_param.shape[0]
        xz = jnp.einsum('bld,ed->ble', x, W_in)
        xc, z = (xz[..., :d_inner], xz[..., d_inner:])
        xt = jnp.swapaxes(xc, 1, 2)
        conv = jax.lax.conv_general_dilated(xt, conv_w, window_strides=(1,), padding=[(conv_w.shape[-1] - 1, 0)], feature_group_count=d_inner, dimension_numbers=('NCH', 'OIH', 'NCH'))
        conv = conv + conv_b[None, :, None]
        u = jax.nn.silu(jnp.swapaxes(conv, 1, 2))
        x_dbl = jnp.einsum('bld,ed->ble', u, W_x)
        dt_raw = x_dbl[..., :1]
        Bp = x_dbl[..., 1:1 + d_state]
        Cp = x_dbl[..., 1 + d_state:]
        dt = jnp.clip(jax.nn.softplus(jnp.einsum('blo,eo->ble', dt_raw, W_dt) + b_dt), 0.0001, 10.0)
        A = -jnp.exp(jnp.minimum(A_log, 5.0))
        y = _selective_scan(u, dt, A, Bp, Cp)
        mu = jnp.mean(y, axis=-1, keepdims=True)
        var = jnp.mean(jnp.square(y - mu), axis=-1, keepdims=True)
        yn = (y - mu) * jax.lax.rsqrt(var + LN_EPS) * ln_g + ln_b
        y = yn + D_param * u
        y = y * jax.nn.silu(z)
        return jnp.einsum('ble,de->bld', y, W_out)

    def _L0_ffn_ref(x, W_r, W_k, W_v, mu_r, mu_k):
        import jax, jax.numpy as jnp
        import numpy as np
        DIM = 256

        def _reference_tuple_inner(x, W_r, W_k, W_v, mu_r, mu_k):
            B, T, C = x.shape
            x_prev = jnp.concatenate([jnp.zeros((B, 1, C), x.dtype), x[:, :-1, :]], axis=1)
            xr = mu_r * x + (1.0 - mu_r) * x_prev
            xk = mu_k * x + (1.0 - mu_k) * x_prev
            r = jax.nn.sigmoid(jnp.einsum('btc,dc->btd', xr, W_r))
            k = jnp.einsum('btc,dc->btd', xk, W_k)
            k_act = jnp.square(jax.nn.relu(k))
            out = r * jnp.einsum('btc,dc->btd', k_act, W_v)
            new_state = x[:, -1, :]
            return (out, new_state)
        return _reference_tuple_inner(x, W_r, W_k, W_v, mu_r, mu_k)[0]
    x = L0_attn_x
    x = x + _L0_attn_ref(_layernorm(x, axis=-1), L0_attn_W_in, L0_attn_conv_w, L0_attn_conv_b, L0_attn_W_x, L0_attn_W_dt, L0_attn_b_dt, L0_attn_A_log, L0_attn_D_param, L0_attn_W_out, L0_attn_ln_g, L0_attn_ln_b)
    x = x + _L0_ffn_ref(_layernorm(x, axis=-1), L0_ffn_W_r, L0_ffn_W_k, L0_ffn_W_v, L0_ffn_mu_r, L0_ffn_mu_k)
    return x

_drawn_inputs = setup_inputs


def setup_inputs(seed=0):
    import zlib

    import numpy as np

    out = dict(_drawn_inputs(seed))
    spreads = {'L0_attn_b_dt': (0.10000000149011612, 0.6),
     'L0_attn_D_param': (1.0, 0.2),
     'L0_attn_ln_g': (1.0, 0.2),
     'L0_attn_ln_b': (0.0, 0.1)}
    factors = {'L0_attn_conv_b': 5.062, 'L0_attn_W_dt': 40.931, 'L0_ffn_W_r': 3.943, 'L0_ffn_mu_r': 7.974}
    for name, (base, spread) in spreads.items():
        noise = np.random.default_rng([zlib.crc32(name.encode()), seed]).standard_normal(out[name].shape)
        drawn = base * np.exp(spread * noise) if base else spread * noise
        out[name] = jnp.asarray(drawn.astype(out[name].dtype))
    for name, factor in factors.items():
        out[name] = (out[name] * factor).astype(out[name].dtype)
    return out
```

```python
import math
from contextlib import ExitStack

SEQS, LEN, DM, DI, NS, TAPS = 16, 512, 256, 512, 16, 4
P = 128
QT = DI // P
KT = DM // P
CH = LEN // P
UNITS = NS * QT
XROWS = NS + 1
LN_EPS = 1e-5
DT_MIN, DT_MAX = 1e-4, 10.0
IN_CLIP, STATE_CLIP, ARG_CLIP = 10.0, 100.0, 20.0
DECAY_MIN = math.exp(-ARG_CLIP)
MARGIN = 0.999
SOFTPLUS_CAP = 1e9
CG = 2
NCG = NS // CG
H_RING = 4
BT_ON_DVE = ()

P_CW, P_CB, P_WDT, P_BDT, P_D, P_G, P_B = 0, 16, 20, 24, 28, 32, 36
P_MR, P_MK, P_N = 40, 42, 44

FRONT = {}
for _name, _slots in (("xT", (5, 6)), ("xc", (8, 10, 12, 14)), ("z", (16, 18, 20, 22)), ("rows", (34,)),
                      ("BT", (36,)), ("duT", (49, 50, 51, 52)), ("uT", (53, 54, 55, 56)),
                      ("bound", (59,)), ("mask", (61,))):
    for _i, _s in enumerate(_slots):
        FRONT[_name, _i] = (len(FRONT), _s)
BACK = {}
for _name, _slots in (("yn", (8, 9, 10, 11)), ("out", (18, 19)), ("x2T", (23, 24)), ("key", (29, 30)),
                      ("rec", (31, 32)), ("val", (36, 37))):
    for _i, _s in enumerate(_slots):
        BACK[_name, _i] = (len(BACK), _s)
NF, NBK = len(FRONT), len(BACK)

BND = 10
BND_ROWS, BND_FLAG = 7, 9


def build(nc, x, w_in, w_x, w_out, w_r, w_k, w_v, params, a_log, ident_in, pow2_in, out, row_scratch):
    import concourse.bass as bass
    from concourse import mybir

    fp32, i32 = mybir.dt.float32, mybir.dt.int32
    ALU = mybir.AluOpType
    ACT = mybir.ActivationFunctionType
    X = mybir.AxisListType.X
    LOGEXP = "natural_log_exp_and_others"

    with ExitStack() as ctx:
        def sb(name, shape, dt=fp32):
            return ctx.enter_context(nc.sbuf_tensor(name, shape, dt))

        def pb(name, shape):
            return ctx.enter_context(nc.psum_tensor(name, shape, fp32))

        def sem(name):
            return ctx.enter_context(nc.semaphore(name))

        win = sb("win", [P, KT, 2 * DI])
        wx = sb("wx", [P, QT, NS + XROWS])
        wout = sb("wout", [P, QT, DM])
        wr = sb("wr", [P, KT, DM])
        wk = sb("wk", [P, KT, DM])
        wv = sb("wv", [P, KT, DM])
        par = sb("par", [P, P_N])
        ident = sb("ident", [P, P])
        pow2 = sb("pow2", [P, 2])
        epst = sb("epst", [P, 1])
        a_pos = sb("a_pos", [P, NS])
        a_neg = sb("a_neg", [P, NS])
        a_inv = sb("a_inv", [P, NS])
        a_lim = sb("a_lim", [P, NS])
        xin = sb("xin", [P, CH, DM])
        xnT = sb("xnT", [P, KT, LEN])
        xc = sb("xc", [P, QT, TAPS - 1 + LEN])
        acc = sb("acc", [P, QT, LEN])
        rows = xin[0:XROWS, 0:2, :].rearrange("p a b -> p (a b)")
        dtrep = xnT[:, 0, :]
        fst = sb("fst", [P, CH, 6])
        fmv = sb("fmv", [P, CH, 2])
        frs = sb("frs", [P, CH])
        babs = sb("babs", [P, CH, NS])
        gb = sb("gb", [P, CH, NS])
        gh = sb("gh", [P, CH, NS])
        um = sb("um", [P, CH])
        dum = sb("dum", [P, CH])
        bound = sb("bound", [P, 2 * NS])
        bmax = sb("bmax", [2 * NS, 1])
        flag = sb("flag", [P, 1])
        u = sb("u", [P, 2, QT, LEN])
        gate = sb("gate", [P, 2, QT, LEN])
        dt = sb("dt", [P, 2, QT, LEN])
        duT = sb("duT", [P, 2, CH, DI])
        BT = sb("BT", [P, 2, CH, NS])
        masks = sb("masks", [1, 2, 2], i32)
        masks_now = sb("masks_now", [1, 2], i32)
        decay = sb("decay", [P, 2, QT, LEN])
        bT = sb("bT", [P, 2, CH, DI])
        h = sb("h", [P, H_RING, QT, LEN])
        cring = sb("cring", [P, 2, CG, LEN])
        hmax = sb("hmax", [P, 32])
        hmaxT = sb("hmaxT", [P, 32])
        hq = sb("hq", [P, 4])
        hover = sb("hover", [1, 1], i32)
        hstep = sb("hstep", [P, 1])
        yT = sb("yT", [P, CH, DI])
        x2n = yT[:, 0:2, :].rearrange("p a (b c) -> p (a b) c", c=DM)
        diff = yT[:, 2:4, :]
        kact = yT[:, 2:4, :]
        e = sb("e", [P, QT, LEN])
        xr = e[:, 0:2, :]
        xk = e[:, 2:4, :]
        x1 = sb("x1", [P, CH, DM])
        x2T = sb("x2T", [P, KT, 1 + LEN])
        rec = x2T[:, :, 1:1 + LEN]
        recT = rec.rearrange("p a (b c) -> p a b c", c=DM)
        bst = sb("bst", [P, CH, 6])
        bmv = sb("bmv", [P, CH, 2])
        brs = sb("brs", [P, CH])

        yps = [pb(f"yps{c}", [P, DI]) for c in range(CH)]
        bps = [pb(f"bps{i}", [P, LEN]) for i in range(2)]
        fps = pb("fps", [P, 512])
        kps = pb("kps", [P, 512])

        w_loaded = sem("w_loaded")
        zeros_set = sem("zeros_set")
        a_cut = sem("a_cut")
        a_exp = sem("a_exp")
        a_done = sem("a_done")
        x_loaded = sem("x_loaded")
        fagg = sem("fagg")
        fln = sem("fln")
        frstd = sem("frstd")
        xn_ready = sem("xn_ready")
        front_full = sem("front_full")
        front_free = sem("front_free")
        conv_step = sem("conv_step")
        u_ready = sem("u_ready")
        gate_ready = sem("gate_ready")
        rows_stored = sem("rows_stored")
        dtrep_loaded = sem("dtrep_loaded")
        dt_exp = sem("dt_exp")
        dt_capped = sem("dt_capped")
        dt_ln = sem("dt_ln")
        dt_ready = sem("dt_ready")
        du_ready = sem("du_ready")
        bnd_step = sem("bnd_step")
        mask_ready = sem("mask_ready")
        c_loaded = [sem(f"c_loaded{i}") for i in range(2)]
        decay_ready = sem("decay_ready")
        bT_act = sem("bT_act")
        bT_dve = sem("bT_dve")
        b_full = sem("b_full")
        h_ready = sem("h_ready")
        p_ready = sem("p_ready")
        p_summed = sem("p_summed")
        yT_act = sem("yT_act")
        yT_dve = sem("yT_dve")
        bagg = sem("bagg")
        bln = sem("bln")
        brstd = sem("brstd")
        yn_ready = sem("yn_ready")
        back_full = sem("back_full")
        back_free = sem("back_free")
        skip_added = sem("skip_added")
        gated = sem("gated")
        xres_loaded = sem("xres_loaded")
        x2n_ready = sem("x2n_ready")
        diff_ready = sem("diff_ready")
        mixed = sem("mixed")
        squared = sem("squared")
        tanh_done = sem("tanh_done")
        val_mul = sem("val_mul")
        out_ready = sem("out_ready")
        stored = sem("stored")

        def cnt(b, per, k):
            return b * per + (k + 1)

        def front_done(b, name, i=0):
            return cnt(b, NF, FRONT[name, i][0])

        def back_done(b, name, i=0):
            return cnt(b, NBK, BACK[name, i][0])

        def static(v):
            return isinstance(v, int)

        def not_first(v, k=0):
            return not static(v) or v + k > 0

        def slots_of(table, name):
            return {s: i for (nm, i), (_, s) in table.items() if nm == name}

        F = {nm: slots_of(FRONT, nm) for nm, _ in FRONT}
        K = {nm: slots_of(BACK, nm) for nm, _ in BACK}

        def periods(eng, body):
            body(0, 0, True, False, False)
            body(1, 1, True, True, False)
            with eng.Fori(1, SEQS // 2) as i:
                for parity in range(2):
                    body(2 * i + parity, parity, True, True, True)
            body(SEQS, 0, False, True, True)
            body(SEQS + 1, 1, False, False, True)

        def weight_loads():
            return ((win, w_in.rearrange("(k p) m -> p k m", p=P)), (wx, w_x.rearrange("(k p) m -> p k m", p=P)),
                    (wout, w_out.rearrange("(k p) m -> p k m", p=P)), (wr, w_r.rearrange("(k p) m -> p k m", p=P)),
                    (wk, w_k.rearrange("(k p) m -> p k m", p=P)), (wv, w_v.rearrange("(k p) m -> p k m", p=P)),
                    (par, params), (ident, ident_in), (pow2, pow2_in), (a_pos, a_log))

        W_ALL = 16 * 10

        block = ctx.enter_context(nc.Block())

        @block.sync
        def _(sp):
            first = True
            for t, src in weight_loads():
                dst = t[:] if len(t.shape) == 2 else t[:, :, :]
                if t is a_pos:
                    src = src.partition_broadcast(P)
                sp.dma_start(dst, src).then_inc(w_loaded, 16)

            def load_c(b, parity, g):
                r = g % 2
                if g >= 2 or not_first(b):
                    sp.wait_ge(p_ready, cnt(b, 2 * NS, 2 * CG * (g - 1) - 1))
                src = row_scratch[parity, CG * g:CG * (g + 1), :].rearrange("a t -> (a t)")
                sp.dma_start(cring[:, r, :, :].rearrange("p a t -> p (a t)"), src.partition_broadcast(P)) \
                    .then_inc(c_loaded[r], 16)

            def body(p, parity, front, units, back):
                fb, ub = p, p - 1
                for s in range(UNITS):
                    if units and s % (UNITS // NCG) == 0 and s // (UNITS // NCG) + 1 < NCG:
                        load_c(ub, 1 - parity, s // (UNITS // NCG) + 1)
                    if front and s == 35:
                        sp.wait_ge(front_free, front_done(fb, "rows"))
                        sp.dma_start(row_scratch[parity], rows).then_inc(rows_stored, 16)
                        sp.wait_ge(rows_stored, 16 * fb + 16)
                        sp.dma_start(dtrep, row_scratch[parity, NS:NS + 1, :].rearrange("a t -> (a t)")
                                     .partition_broadcast(P)).then_inc(dtrep_loaded, 16)
                if front:
                    load_c(fb, parity, 0)

            periods(sp, body)
            sp.wait_ge(rows_stored, 16 * SEQS)

        @block.tensor
        def _(pe):
            pe.wait_ge(w_loaded, W_ALL)

            def turn(dst, src, start=True, stop=True):
                return nc.tensor.matmul(dst, src, ident[0:src.shape[0], 0:src.shape[0]], start=start, stop=stop,
                                        is_transpose=True, skip_group_check=True)

            def unit_input(b, n, q):
                k = QT * n + q
                if n > 1 or (k > 1) or not_first(b):
                    if k >= 2 or not_first(b):
                        pe.wait_ge(h_ready, cnt(b, UNITS, k - 2))
                if q == 0:
                    if len(BT_ON_DVE) < CH:
                        pe.wait_ge(bT_act, cnt(b, NS, n))
                    if BT_ON_DVE:
                        pe.wait_ge(bT_dve, cnt(b, NS, n))
                for c in range(CH):
                    last = turn(bps[k % 2][:, c * P:(c + 1) * P], bT[:, n % 2, c, q * P:(q + 1) * P])
                last.then_inc(b_full, 1)

            def unit_sum(b, n, q):
                if q % 2 == 0:
                    pe.wait_ge(p_ready, cnt(b, 2 * NS, 2 * n + q // 2))
                if n == 0 and q == 0 and not_first(b):
                    pe.wait_ge(yT_act, 2 * b)
                    pe.wait_ge(yT_dve, 2 * b)
                for c in range(CH):
                    last = turn(yps[c][:, q * P:(q + 1) * P], h[:, n % H_RING, q, c * P:(c + 1) * P],
                                start=(n == 0 and q == 0), stop=(n == NS - 1))
                last.then_inc(p_summed, 1)

            def front_bank(b, name, i=0):
                k = FRONT[name, i][0]
                if k > 0 or not_first(b):
                    pe.wait_ge(front_free, cnt(b, NF, k - 1))

            def back_bank(b, name, i=0):
                k = BACK[name, i][0]
                if k > 0 or not_first(b):
                    pe.wait_ge(back_free, cnt(b, NBK, k - 1))

            def front_step(b, parity, s):
                if s in F["xT"]:
                    k = F["xT"][s]
                    front_bank(b, "xT", k)
                    pe.wait_ge(xn_ready, b + 1)
                    for c in range(CH):
                        last = turn(fps[:, c * P:(c + 1) * P], xin[:, c, k * P:(k + 1) * P])
                    last.then_inc(front_full, 1)
                for name, first in (("xc", 0), ("z", QT)):
                    if s in F[name]:
                        m = F[name][s]
                        front_bank(b, name, m)
                        for k in range(KT):
                            last = nc.tensor.matmul(fps[:, :], win[:, k, (first + m) * P:(first + m + 1) * P],
                                                    xnT[:, k, :], start=(k == 0), stop=(k == KT - 1))
                        last.then_inc(front_full, 1)
                if s in F["rows"]:
                    front_bank(b, "rows")
                    pe.wait_ge(u_ready, b + 1)
                    for k in range(QT):
                        last = nc.tensor.matmul(fps[0:XROWS, :], wx[:, k, NS:], u[:, parity, k, :],
                                                start=(k == 0), stop=(k == QT - 1))
                    last.then_inc(front_full, 1)
                if s in F["BT"]:
                    front_bank(b, "BT")
                    for c in range(CH):
                        for k in range(QT):
                            last = nc.tensor.matmul(fps[:, c * NS:(c + 1) * NS], u[:, parity, k, c * P:(c + 1) * P],
                                                    wx[:, k, 0:NS], start=(k == 0), stop=(k == QT - 1))
                    last.then_inc(front_full, 1)
                if s in F["duT"]:
                    c = F["duT"][s]
                    front_bank(b, "duT", c)
                    pe.wait_ge(du_ready, b + 1)
                    for q in range(QT):
                        last = turn(fps[:, q * P:(q + 1) * P], acc[:, q, c * P:(c + 1) * P])
                    last.then_inc(front_full, 1)
                if s in F["uT"]:
                    c = F["uT"][s]
                    front_bank(b, "uT", c)
                    for q in range(QT):
                        last = turn(fps[:, q * P:(q + 1) * P], u[:, parity, q, c * P:(c + 1) * P])
                    last.then_inc(front_full, 1)
                if s in F["bound"]:
                    front_bank(b, "bound")
                    pe.wait_ge(bnd_step, cnt(b, BND, BND_ROWS))
                    turn(fps[0:2 * NS, 0:P], bound[:, :]).then_inc(front_full, 1)
                if s in F["mask"]:
                    front_bank(b, "mask")
                    pe.wait_ge(bnd_step, cnt(b, BND, BND_FLAG))
                    nc.tensor.matmul(fps[0:1, 0:2], flag[:, :], pow2[:, :], start=True, stop=True) \
                        .then_inc(front_full, 1)

            def back_step(b, s):
                if s in K["yn"]:
                    q = K["yn"][s]
                    back_bank(b, "yn", q)
                    pe.wait_ge(yn_ready, b + 1)
                    for c in range(CH):
                        last = turn(kps[:, c * P:(c + 1) * P], yT[:, c, q * P:(q + 1) * P])
                    last.then_inc(back_full, 1)
                if s in K["out"]:
                    j = K["out"][s]
                    back_bank(b, "out", j)
                    pe.wait_ge(gated, b + 1)
                    for c in range(2):
                        t = 2 * j + c
                        for k in range(QT):
                            last = nc.tensor.matmul(kps[:, c * DM:(c + 1) * DM], e[:, k, t * P:(t + 1) * P],
                                                    wout[:, k, :], start=(k == 0), stop=(k == QT - 1))
                    last.then_inc(back_full, 1)
                if s in K["x2T"]:
                    k = K["x2T"][s]
                    back_bank(b, "x2T", k)
                    pe.wait_ge(x2n_ready, b + 1)
                    for c in range(CH):
                        last = turn(kps[:, c * P:(c + 1) * P], x2n[:, c, k * P:(k + 1) * P])
                    last.then_inc(back_full, 1)
                if s in K["key"]:
                    m = K["key"][s]
                    back_bank(b, "key", m)
                    pe.wait_ge(mixed, 2 * b + 2)
                    for k in range(KT):
                        last = nc.tensor.matmul(kps[:, :], wk[:, k, m * P:(m + 1) * P], xk[:, k, :],
                                                start=(k == 0), stop=(k == KT - 1))
                    last.then_inc(back_full, 1)
                for name, w, act in (("rec", wr, xr), ("val", wv, kact)):
                    if s in K[name]:
                        j = K[name][s]
                        back_bank(b, name, j)
                        if name == "val":
                            pe.wait_ge(squared, b + 1)
                        for c in range(2):
                            t = 2 * j + c
                            for k in range(KT):
                                last = nc.tensor.matmul(kps[:, c * DM:(c + 1) * DM], act[:, k, t * P:(t + 1) * P],
                                                        w[:, k, :], start=(k == 0), stop=(k == KT - 1))
                        last.then_inc(back_full, 1)

            def body(p, parity, front, units, back):
                for s in range(UNITS):
                    n, q = divmod(s, QT)
                    if units:
                        unit_input(p - 1, n, q)
                    if n > 0 and units:
                        unit_sum(p - 1, n - 1, q)
                    elif n == 0 and back:
                        unit_sum(p - 2, NS - 1, q)
                    if front:
                        front_step(p, parity, s)
                    if back:
                        back_step(p - 2, s)

            periods(pe, body)

        @block.scalar
        def _(act):
            nc.scalar.preload_act_table_set(LOGEXP)
            act.wait_ge(a_cut, 1)
            nc.scalar.activation(a_pos[:, :], a_pos[:, :], ACT.Exp).then_inc(a_exp, 1)
            act.wait_ge(a_done, 1)

            def unit_terms(b, parity, n, c):
                if c == 0:
                    if n >= 2 or not_first(b):
                        act.wait_ge(h_ready, cnt(b, UNITS, QT * (n - 1) - 1))
                    if n == 0:
                        act.wait_ge(dt_ready, b + 1)
                    nc.scalar.activation(decay[:, n % 2, :, :], dt[:, parity, :, :], ACT.Exp,
                                         scale=a_neg[:, n:n + 1]).then_inc(decay_ready, 1)
                    if n >= 2 or not_first(b):
                        act.wait_ge(b_full, cnt(b, UNITS, QT * (n - 1) - 1))
                    if n == 0:
                        act.wait_ge(front_free, front_done(b, "duT", CH - 1))
                if c in BT_ON_DVE:
                    return
                mine = [k for k in range(CH) if k not in BT_ON_DVE]
                ins = nc.scalar.activation(bT[:, n % 2, c, :], duT[:, parity, c, :], ACT.Copy,
                                           scale=BT[:, parity, c, n:n + 1])
                if c == mine[-1]:
                    ins.then_inc(bT_act, 1)

            def rstd(mv, rs, ln_sem, done_sem, value):
                nc.scalar.activation(rs[:, :], mv[:, :, 1], ACT.Ln, bias=epst[:, 0:1]).then_inc(ln_sem, 1)
                act.wait_ge(ln_sem, value)
                nc.scalar.activation(rs[:, :], rs[:, :], ACT.Exp, scale=-0.5).then_inc(done_sem, 1)

            def front_step(b, parity, s):
                def ready(name, i=0):
                    act.wait_ge(front_full, front_done(b, name, i))
                if s == 2:
                    act.wait_ge(fagg, b + 1)
                    rstd(fmv, frs, fln, frstd, b + 1)
                if s in F["xT"]:
                    k = F["xT"][s]
                    ready("xT", k)
                    if k == 0 and not_first(b):
                        act.wait_ge(dt_exp, b)
                    nc.scalar.activation(xnT[:, k, :], fps[:, :], ACT.Copy).then_inc(front_free, 1)
                if s in F["xc"]:
                    m = F["xc"][s]
                    ready("xc", m)
                    nc.scalar.activation(xc[:, m, TAPS - 1:], fps[:, :], ACT.Copy).then_inc(front_free, 1)
                if s in F["z"]:
                    m = F["z"][s]
                    ready("z", m)
                    if m == 0 and (not_first(b, -1)):
                        act.wait_ge(gated, b - 1)
                    nc.scalar.activation(gate[:, parity, m, :], fps[:, :], ACT.Copy).then_inc(front_free, 1)
                if s in F["rows"]:
                    ready("rows")
                    nc.scalar.activation(rows[:, :], fps[0:XROWS, :], ACT.Copy).then_inc(front_free, 1)
                if s in F["BT"]:
                    ready("BT")
                    nc.scalar.activation(BT[:, parity, :, :], fps[:, 0:CH * NS].rearrange("p (c n) -> p c n", n=NS),
                                         ACT.Copy).then_inc(front_free, 1)
                if s == 39:
                    act.wait_ge(dtrep_loaded, 16 * b + 16)
                    for q in range(QT):
                        last = nc.scalar.activation(dt[:, parity, q, :], dtrep, ACT.Exp,
                                                    scale=par[:, P_WDT + q:P_WDT + q + 1],
                                                    bias=par[:, P_BDT + q:P_BDT + q + 1])
                    last.then_inc(dt_exp, 1)
                if s == 41:
                    act.wait_ge(dt_capped, b + 1)
                    nc.scalar.activation(dt[:, parity, :, :], dt[:, parity, :, :], ACT.Ln, bias=1.0) \
                        .then_inc(dt_ln, 1)
                if s in F["duT"]:
                    c = F["duT"][s]
                    ready("duT", c)
                    nc.scalar.activation(duT[:, parity, c, :], fps[:, :], ACT.Copy).then_inc(front_free, 1)

            def back_step(b, s):
                def ready(name, i=0):
                    act.wait_ge(back_full, back_done(b, name, i))
                if s == 4:
                    act.wait_ge(p_summed, UNITS * b + UNITS)
                    for c in range(2):
                        nc.scalar.activation(yT[:, c, :], yps[c][:, :], ACT.Copy).then_inc(yT_act, 1)
                if s == 6:
                    act.wait_ge(bagg, 2 * b + 1)
                    rstd(bmv, brs, bln, brstd, 2 * b + 1)
                if s in K["yn"]:
                    q = K["yn"][s]
                    ready("yn", q)
                    nc.scalar.activation(e[:, q, :], kps[:, :], ACT.Identity, scale=par[:, P_G + q:P_G + q + 1],
                                         bias=par[:, P_B + q:P_B + q + 1]).then_inc(back_free, 1)
                if s == 21:
                    act.wait_ge(bagg, 2 * b + 2)
                    rstd(bmv, brs, bln, brstd, 2 * b + 2)
                if s in K["x2T"]:
                    k = K["x2T"][s]
                    ready("x2T", k)
                    nc.scalar.activation(x2T[:, k, 1:], kps[:, :], ACT.Copy).then_inc(back_free, 1)
                if s in K["key"]:
                    m = K["key"][s]
                    ready("key", m)
                    nc.scalar.activation(kact[:, m, :], kps[:, :], ACT.Relu).then_inc(back_free, 1)
                if s in K["rec"]:
                    j = K["rec"][s]
                    ready("rec", j)
                    nc.scalar.activation(rec[:, j, :], kps[:, :], ACT.Copy).then_inc(back_free, 1)

            def nonlinear(p, parity, front, back):
                if front:
                    act.wait_ge(conv_step, cnt(p, TAPS, TAPS - 1))
                    nc.scalar.activation(u[:, parity, :, :], acc[:, :, :], ACT.Silu).then_inc(u_ready, 1)
                    act.wait_ge(front_free, front_done(p, "z", QT - 1))
                    nc.scalar.activation(gate[:, parity, :, :], gate[:, parity, :, :], ACT.Silu) \
                        .then_inc(gate_ready, 1)
                if back:
                    act.wait_ge(back_free, back_done(p - 2, "rec", 1))
                    nc.scalar.activation(rec, rec, ACT.Tanh, scale=0.5).then_inc(tanh_done, 1)
                nc.scalar.preload_act_table_set(LOGEXP)

            def in_chunks(t):
                return t.rearrange("(c t) d -> t c d", t=P)

            def load_x(fb, kb, front, back):
                if front:
                    if not_first(fb):
                        act.wait_ge(front_free, front_done(fb - 1, "BT"))
                        act.wait_ge(rows_stored, 16 * fb)
                    act.dma_start(xin[:, :, :], in_chunks(x[fb])).then_inc(x_loaded, 16)
                if back:
                    if not_first(kb):
                        act.wait_ge(stored, 16 * kb)
                    act.dma_start(x1[:, :, :], in_chunks(x[kb])).then_inc(xres_loaded, 16)

            def body(p, parity, front, units, back):
                load_x(p, p - 2, front, back)
                if units:
                    for c in range(CH):
                        unit_terms(p - 1, 1 - parity, 0, c)
                for s in range(UNITS):
                    n, c = divmod(s, CH)
                    if units and n + 1 < NS:
                        unit_terms(p - 1, 1 - parity, n + 1, c)
                    if back:
                        back_step(p - 2, s)
                    if front:
                        front_step(p, parity, s)
                    if s == 32:
                        nonlinear(p, parity, front, back)
                    if back and s == 44:
                        act.wait_ge(out_ready, p - 1)
                        act.dma_start(in_chunks(out[p - 2]), x1[:, :, :]).then_inc(stored, 16)

            periods(act, body)
            act.wait_ge(stored, 16 * SEQS)

        @block.gpsimd
        def _(pool):
            nc.gpsimd.memset(xc[:, :, 0:TAPS - 1], 0.0).then_inc(zeros_set, 1)
            nc.gpsimd.memset(x2T[:, :, 0:1], 0.0).then_inc(zeros_set, 1)
            nc.gpsimd.memset(hmax[:, :], 0.0).then_inc(zeros_set, 1)
            nc.gpsimd.memset(epst[:, :], LN_EPS).then_inc(zeros_set, 1)
            nc.gpsimd.memset(flag[:, :], 0.0).then_inc(zeros_set, 1)
            pool.wait_ge(zeros_set, 5)

            def unit_product(b, n, half):
                if half == 0 and n % CG == 0:
                    g = n // CG
                    pool.wait_ge(c_loaded[g % 2], cnt(b, NCG // 2, g // 2) * 16)
                pool.wait_ge(h_ready, cnt(b, UNITS, QT * n + 2 * half + 1))
                hs = h[:, n % H_RING, 2 * half:2 * half + 2, :]
                cs = cring[:, (n // CG) % 2, n % CG:n % CG + 1, :].broadcast_to([P, 2, LEN])
                nc.gpsimd.tensor_tensor(hs, hs, cs, ALU.mult).then_inc(p_ready, 1)

            def body(p, parity, front, units, back):
                for s in range(UNITS):
                    n, q = divmod(s, QT)
                    if units and q % 2 == 1:
                        unit_product(p - 1, n, q // 2)
                    if back and s == 14:
                        pool.wait_ge(skip_added, p - 1)
                        pool.wait_ge(gate_ready, p - 1)
                        nc.gpsimd.tensor_tensor(e[:, :, :], e[:, :, :], gate[:, parity, :, :], ALU.mult) \
                            .then_inc(gated, 1)
                    if back and s == 25:
                        pool.wait_ge(back_free, back_done(p - 2, "x2T", 1))
                        nc.gpsimd.tensor_tensor(diff, x2T[:, :, 1:], x2T[:, :, 0:LEN], ALU.subtract) \
                            .then_inc(diff_ready, 1)
                    if back and s == 32:
                        pool.wait_ge(back_free, back_done(p - 2, "key", 1))
                        nc.gpsimd.tensor_tensor(kact, kact, kact, ALU.mult).then_inc(squared, 1)
                    if front and s == 43:
                        pool.wait_ge(dt_ready, p + 1)
                        pool.wait_ge(u_ready, p + 1)
                        nc.gpsimd.tensor_tensor(acc[:, :, :], dt[:, parity, :, :], u[:, parity, :, :], ALU.mult) \
                            .then_inc(du_ready, 1)

            periods(pool, body)

        @block.vector
        def _(dve):
            V = nc.vector
            dve.wait_ge(w_loaded, W_ALL)
            dve.wait_ge(zeros_set, 5)
            V.tensor_scalar(a_pos[:, :], a_pos[:, :], 5.0, None, ALU.min).then_inc(a_cut, 1)
            dve.wait_ge(a_exp, 1)
            V.reciprocal(a_inv[:, :], a_pos[:, :])
            V.tensor_scalar(a_lim[:, :], a_pos[:, :], DT_MAX / ARG_CLIP / MARGIN, None, ALU.mult)
            V.tensor_scalar(a_neg[:, :], a_pos[:, :], -1.0, None, ALU.mult).then_inc(a_done, 1)
            dve.wait_ge(a_done, 1)

            def scan(n, q):
                return V.tensor_tensor_scan(h[:, n % H_RING, q, :], decay[:, n % 2, q, :],
                                            bps[(QT * n + q) % 2][:, :], 0.0, ALU.mult, ALU.add)

            def clipped_steps(n, q):
                hq_, dq_, bq_ = h[:, n % H_RING, q, :], decay[:, n % 2, q, :], bps[(QT * n + q) % 2]
                V.tensor_scalar(hq_[:, 0:1], bq_[:, 0:1], STATE_CLIP, -STATE_CLIP, ALU.min, ALU.max)
                dve.drain()
                with dve.Fori(1, LEN) as t:
                    V.scalar_tensor_tensor(hstep[:, :], hq_[:, bass.ds(t - 1, 1)], dq_[:, bass.ds(t, 1)],
                                           bq_[:, bass.ds(t, 1)], ALU.mult, ALU.add)
                    dve.drain()
                    V.tensor_scalar(hq_[:, bass.ds(t, 1)], hstep[:, :], STATE_CLIP, -STATE_CLIP, ALU.min, ALU.max)
                    dve.drain()

            def state_over_clip(n, q):
                V.tensor_reduce(hmax[:, 0:1], h[:, n % H_RING, q, :], X, ALU.max, apply_absolute_value=True)
                dve.drain()
                V.transpose(hmaxT[:, :], hmax[:, :])
                dve.drain()
                for k in range(4):
                    V.tensor_reduce(hq[0:1, k:k + 1], hmaxT[32 * k:32 * k + 1, :], X, ALU.max)
                dve.drain()
                V.tensor_reduce(hstep[0:1, :], hq[0:1, :], X, ALU.max)
                dve.drain()
                V.tensor_scalar(hover[:, :], hstep[0:1, :], STATE_CLIP, None, ALU.is_gt)
                dve.drain()
                return dve.value_load(hover[0:1, 0:1], min_val=0, max_val=1)

            def unit_scan(b, n, q, clip_mask, state_mask):
                k = QT * n + q

                def inputs_ready():
                    if q == 0:
                        dve.wait_ge(decay_ready, cnt(b, NS, n))
                    if n >= H_RING or not_first(b):
                        dve.wait_ge(p_summed, cnt(b, UNITS, k - QT * H_RING))
                    dve.wait_ge(b_full, cnt(b, UNITS, k))

                with dve.If(((clip_mask >> n) & 1) > 0):
                    inputs_ready()
                    bk, dk = bps[k % 2], decay[:, n % 2, q, :]
                    V.tensor_scalar(bk[:, :], bk[:, :], IN_CLIP, -IN_CLIP, ALU.min, ALU.max)
                    V.tensor_scalar(dk, dk, DECAY_MIN, None, ALU.max)
                    dve.drain()
                    scan(n, q)
                    dve.drain()
                    with dve.If(((state_mask >> n) & 1) > 0):
                        over = state_over_clip(n, q)
                        with dve.If(over > 0):
                            clipped_steps(n, q)
                    dve.sem_inc(h_ready, 1)
                with dve.Else():
                    inputs_ready()
                    scan(n, q).then_inc(h_ready, 1)

            def bT_share(b, parity, n, c):
                if c == BT_ON_DVE[0] and (n >= 2 or not_first(b)):
                    dve.wait_ge(b_full, cnt(b, UNITS, QT * (n - 1) - 1))
                if n == 0:
                    dve.wait_ge(front_free, front_done(b, "duT", CH - 1))
                ins = V.tensor_scalar(bT[:, n % 2, c, :], duT[:, parity, c, :], BT[:, parity, c, n:n + 1], None,
                                      ALU.mult)
                if c == BT_ON_DVE[-1]:
                    ins.then_inc(bT_dve, 1)

            def stats(st, mv, src, agg_sem):
                for c in range(CH):
                    last = V.bn_stats(st[:, c, :], src[:, c, :])
                dve.drain()
                for c in range(CH):
                    last = V.bn_aggr(mv[:, c, :], st[:, c, :])
                last.then_inc(agg_sem, 1)

            def normalise(dst, src, mv, rs, done_sem):
                for c in range(CH):
                    last = V.tensor_scalar(dst[:, c, :], src[:, c, :], mv[:, c, 0:1], rs[:, c:c + 1],
                                           ALU.subtract, ALU.mult)
                last.then_inc(done_sem, 1)

            def front_step(b, parity, s):
                if s == 1:
                    dve.wait_ge(x_loaded, 16 * b + 16)
                    if not_first(b):
                        dve.wait_ge(frstd, b)
                    stats(fst, fmv, xin, fagg)
                if s == 3:
                    dve.wait_ge(frstd, b + 1)
                    normalise(xin, xin, fmv, frs, xn_ready)
                if s in (15, 17, 20, 22):
                    tap = (15, 17, 20, 22).index(s)
                    w = TAPS - 1 - tap
                    if tap == 0:
                        dve.wait_ge(front_free, front_done(b, "xc", QT - 1))
                        if not_first(b):
                            dve.wait_ge(front_free, front_done(b - 1, "duT", CH - 1))
                    else:
                        dve.wait_ge(conv_step, cnt(b, TAPS, tap - 1))
                    for q in range(QT):
                        wcol = par[:, P_CW + TAPS * q + w:P_CW + TAPS * q + w + 1]
                        if tap == 0:
                            last = V.tensor_scalar(acc[:, q, :], xc[:, q, w:w + LEN], wcol,
                                                   par[:, P_CB + q:P_CB + q + 1], ALU.mult, ALU.add)
                        else:
                            last = V.scalar_tensor_tensor(acc[:, q, :], xc[:, q, w:w + LEN], wcol, acc[:, q, :],
                                                          ALU.mult, ALU.add)
                    last.then_inc(conv_step, 1)
                if s == 40:
                    dve.wait_ge(dt_exp, b + 1)
                    V.tensor_scalar(dt[:, parity, :, :], dt[:, parity, :, :], SOFTPLUS_CAP, None, ALU.min) \
                        .then_inc(dt_capped, 1)
                if s == 42:
                    dve.wait_ge(dt_ln, b + 1)
                    V.tensor_scalar(dt[:, parity, :, :], dt[:, parity, :, :], DT_MIN, DT_MAX, ALU.max, ALU.min) \
                        .then_inc(dt_ready, 1)
                if s == 53:
                    dve.wait_ge(front_free, front_done(b, "duT", CH - 1))
                    V.tensor_reduce(dum[:, :], duT[:, parity, :, :], X, ALU.max, apply_absolute_value=True) \
                        .then_inc(bnd_step, 1)
                    V.tensor_scalar(babs[:, :, :], BT[:, parity, :, :], -1.0, None, ALU.mult).then_inc(bnd_step, 1)
                if s in F["uT"]:
                    c = F["uT"][s]
                    dve.wait_ge(front_full, front_done(b, "uT", c))
                    V.tensor_reduce(um[:, c:c + 1], fps[:, :], X, ALU.max, apply_absolute_value=True) \
                        .then_inc(front_free, 1)
                if s == 57:
                    bc = [P, CH, NS]
                    dve.wait_ge(bnd_step, cnt(b, BND, 1))
                    V.tensor_tensor(babs[:, :, :], babs[:, :, :], BT[:, parity, :, :], ALU.max).then_inc(bnd_step, 1)
                    dve.wait_ge(bnd_step, cnt(b, BND, 2))
                    V.tensor_tensor(gb[:, :, :], babs[:, :, :], dum[:, :].unsqueeze(2).broadcast_to(bc), ALU.mult) \
                        .then_inc(bnd_step, 1)
                    dve.wait_ge(front_free, front_done(b, "uT", CH - 1))
                    V.tensor_tensor(gh[:, :, :], babs[:, :, :], um[:, :].unsqueeze(2).broadcast_to(bc), ALU.mult) \
                        .then_inc(bnd_step, 1)
                    dve.wait_ge(bnd_step, cnt(b, BND, 4))
                    V.tensor_tensor(gh[:, :, :], gh[:, :, :], a_inv[:, :].unsqueeze(1).broadcast_to(bc), ALU.mult) \
                        .then_inc(bnd_step, 1)
                    dve.wait_ge(bnd_step, cnt(b, BND, 5))
                    V.tensor_tensor(gh[:, :, :], gh[:, :, :], gb[:, :, :], ALU.add).then_inc(bnd_step, 1)
                if s == 58:
                    dve.wait_ge(bnd_step, cnt(b, BND, 6))
                    V.tensor_reduce(bound[:, 0:NS], gb[:, :, :].rearrange("p c n -> p n c"), X, ALU.max)
                    V.tensor_reduce(bound[:, NS:2 * NS], gh[:, :, :].rearrange("p c n -> p n c"), X, ALU.max)
                    dve.drain()
                    V.tensor_scalar(bound[:, 0:NS], bound[:, 0:NS], 1.0 / (IN_CLIP * MARGIN), None, ALU.mult)
                    V.tensor_scalar(bound[:, NS:2 * NS], bound[:, NS:2 * NS], 1.0 / (STATE_CLIP * MARGIN), None,
                                    ALU.mult)
                    dve.drain()
                    V.tensor_tensor(bound[:, 0:NS], bound[:, 0:NS], bound[:, NS:2 * NS], ALU.max)
                    dve.drain()
                    V.tensor_tensor(bound[:, 0:NS], bound[:, 0:NS], a_lim[:, :], ALU.max).then_inc(bnd_step, 1)
                if s in F["bound"]:
                    dve.wait_ge(front_full, front_done(b, "bound"))
                    V.tensor_reduce(bmax[:, :], fps[0:2 * NS, 0:P], X, ALU.max).then_inc(bnd_step, 1)
                    dve.wait_ge(bnd_step, cnt(b, BND, 8))
                    V.tensor_scalar(flag[0:2 * NS, :], bmax[:, :], 1.0, None, ALU.is_gt).then_inc(bnd_step, 1)
                    dve.sem_inc(front_free, 1)
                if s in F["mask"]:
                    dve.wait_ge(front_full, front_done(b, "mask"))
                    V.tensor_copy(masks[0:1, parity, :], fps[0:1, 0:2]).then_inc(front_free, 1)

            def back_step(b, parity, s):
                if s == 4:
                    dve.wait_ge(p_summed, UNITS * b + UNITS)
                    for c in range(2, CH):
                        V.tensor_copy(yT[:, c, :], yps[c][:, :]).then_inc(yT_dve, 1)
                if s == 5:
                    dve.wait_ge(yT_act, 2 * b + 2)
                    dve.wait_ge(yT_dve, 2 * b + 2)
                    stats(bst, bmv, yT, bagg)
                if s == 7:
                    dve.wait_ge(brstd, 2 * b + 1)
                    normalise(yT, yT, bmv, brs, yn_ready)
                if s in (9, 10, 11, 12):
                    q = s - 9
                    dve.wait_ge(back_free, back_done(b, "yn", q))
                    ins = V.scalar_tensor_tensor(e[:, q, :], u[:, parity, q, :], par[:, P_D + q:P_D + q + 1],
                                                 e[:, q, :], ALU.mult, ALU.add)
                    if q == QT - 1:
                        ins.then_inc(skip_added, 1)
                if s in K["out"]:
                    j = K["out"][s]
                    dve.wait_ge(back_full, back_done(b, "out", j))
                    dve.wait_ge(xres_loaded, 16 * b + 16)
                    xs = x1[:, 2 * j:2 * j + 2, :]
                    V.tensor_tensor(xs, kps[:, :].rearrange("p (c d) -> p c d", d=DM), xs, ALU.add) \
                        .then_inc(back_free, 1)
                if s == 20:
                    dve.wait_ge(back_free, back_done(b, "out", 1))
                    stats(bst, bmv, x1, bagg)
                if s == 22:
                    dve.wait_ge(brstd, 2 * b + 2)
                    normalise(x2n, x1, bmv, brs, x2n_ready)
                if s in (27, 28):
                    if s == 27:
                        dve.wait_ge(diff_ready, b + 1)
                    dst, col = ((xr, P_MR), (xk, P_MK))[s - 27]
                    for k in range(KT):
                        last = V.scalar_tensor_tensor(dst[:, k, :], diff[:, k, :], par[:, col + k:col + k + 1],
                                                      x2T[:, k, 0:LEN], ALU.mult, ALU.add)
                    last.then_inc(mixed, 1)
                if s in K["val"]:
                    j = K["val"][s]
                    dve.wait_ge(back_full, back_done(b, "val", j))
                    dve.wait_ge(tanh_done, b + 1)
                    V.scalar_tensor_tensor(rec[:, j, :], rec[:, j, :], 1.0, kps[:, :], ALU.add, ALU.mult) \
                        .then_inc(back_free, 1)
                if s == 39:
                    dve.wait_ge(back_free, back_done(b, "val", 1))
                    x1h = x1[:, :, :].rearrange("p (a c) d -> p a (c d)", a=2)
                    V.scalar_tensor_tensor(x1h, rec, 0.5, x1h, ALU.mult, ALU.add).then_inc(out_ready, 1)

            def body(p, parity, front, units, back):
                if units:
                    dve.wait_ge(front_free, front_done(p - 1, "mask"))
                    V.tensor_copy(masks_now[0:1, :], masks[0:1, 1 - parity, :])
                    dve.drain()
                    clip_mask = dve.value_load(masks_now[0:1, 0:1], min_val=0, max_val=2 ** NS - 1)
                    state_mask = dve.value_load(masks_now[0:1, 1:2], min_val=0, max_val=2 ** NS - 1)
                    for c in BT_ON_DVE:
                        bT_share(p - 1, 1 - parity, 0, c)
                for s in range(UNITS):
                    n, q = divmod(s, QT)
                    if units:
                        unit_scan(p - 1, n, q, clip_mask, state_mask)
                        if q in BT_ON_DVE and n + 1 < NS:
                            bT_share(p - 1, 1 - parity, n + 1, q)
                    if back:
                        back_step(p - 2, parity, s)
                    if front:
                        front_step(p, parity, s)

            periods(dve, body)


def kernel(L0_attn_x, L0_attn_W_in, L0_attn_conv_w, L0_attn_conv_b, L0_attn_W_x, L0_attn_W_dt, L0_attn_b_dt,
           L0_attn_A_log, L0_attn_D_param, L0_attn_W_out, L0_attn_ln_g, L0_attn_ln_b, L0_ffn_W_r, L0_ffn_W_k,
           L0_ffn_W_v, L0_ffn_mu_r, L0_ffn_mu_k):
    import numpy as np
    import concourse.bacc as bacc
    from concourse import mybir
    from concourse.bass_utils import run_bass_kernel_spmd

    def cols(v, n):
        return np.ascontiguousarray(np.asarray(v).reshape(n, P).T)

    conv = np.asarray(L0_attn_conv_w).reshape(QT, P, TAPS).transpose(1, 0, 2).reshape(P, QT * TAPS)
    params = np.concatenate([conv] + [cols(v, QT) for v in (L0_attn_conv_b, L0_attn_W_dt, L0_attn_b_dt,
                                                            L0_attn_D_param, L0_attn_ln_g, L0_attn_ln_b)]
                            + [cols(v, KT) for v in (L0_ffn_mu_r, L0_ffn_mu_k)], axis=1)
    w_x = np.asarray(L0_attn_W_x)
    pow2 = np.zeros((P, 2), np.float32)
    for n in range(NS):
        pow2[n, 0] = pow2[NS + n, 1] = 2.0 ** n
    arrays = {
        "x": np.asarray(L0_attn_x), "w_in": np.asarray(L0_attn_W_in).T,
        "w_x": np.concatenate([w_x[1:], w_x[:1]], axis=0).T, "w_out": np.asarray(L0_attn_W_out).T,
        "w_r": np.asarray(L0_ffn_W_r).T, "w_k": np.asarray(L0_ffn_W_k).T, "w_v": np.asarray(L0_ffn_W_v).T,
        "params": params, "a_log": np.asarray(L0_attn_A_log),
        "ident": np.eye(P, dtype=np.float32), "pow2": pow2,
    }
    nc = bacc.Bacc("TRN2", target_bir_lowering=False, num_devices=1)
    fp32 = mybir.dt.float32
    ins = {f"{k}_dram": np.ascontiguousarray(v) for k, v in arrays.items()}
    aps = [nc.dram_tensor(k, v.shape, fp32, kind="ExternalInput").ap() for k, v in ins.items()]
    out = nc.dram_tensor("out_dram", (SEQS, LEN, DM), fp32, kind="ExternalOutput").ap()
    scratch = nc.dram_tensor("row_scratch", (2, NS + 1, LEN), fp32, kind="Internal").ap()
    build(nc, *aps, out, scratch)
    return run_bass_kernel_spmd(nc, [ins], core_ids=[0]).results[0]["out_dram"]
```

```python
import math
from contextlib import ExitStack

SEQS, LEN, DM, DI, NS, TAPS = 16, 512, 256, 512, 16, 4
P = 128
QT = DI // P
KT = DM // P
CH = LEN // P
UNITS = NS * QT
XROWS = 2 * NS + 1
LN_EPS = 1e-5
DT_MIN, DT_MAX = 1e-4, 10.0
IN_CLIP, STATE_CLIP, ARG_CLIP = 10.0, 100.0, 20.0
DECAY_MIN = math.exp(-ARG_CLIP)
MARGIN = 0.995
B_LOW_CAP = 9.9
SOFTPLUS_CAP = 1e9
R_MIN = -43.0
CG = 2
NCG = NS // CG
H_RING = 4
SUM_LAG = 2
BT_ON_DVE = (9,)
BT_ON_ACT = tuple(n for n in range(NS) if n not in BT_ON_DVE)
CONV_SLOT = 13

P_CW, P_CB, P_WDT, P_BDT, P_D, P_G, P_B = 0, 16, 20, 24, 28, 32, 36
P_MR, P_MK, P_N = 40, 42, 44

FRONT = {}
for _name, _slots in (("xT", (6, 7)), ("xc", (8, 10, 12, 14)), ("z", (28, 29, 30, 31)), ("rows", (37,)),
                      ("BT", (39,)), ("duT", (52, 53, 54, 56)), ("beta", (59,)), ("mask", (61,))):
    for _i, _s in enumerate(_slots):
        FRONT[_name, _i] = (len(FRONT), _s)
BACK = {}
for _name, _slots in (("yn", (17, 18, 19, 20)), ("out", (32, 33)), ("x2T", (40, 41)), ("key", (47, 48)),
                      ("rec", (50, 51)), ("val", (58, 59))):
    for _i, _s in enumerate(_slots):
        BACK[_name, _i] = (len(BACK), _s)
NF, NBK = len(FRONT), len(BACK)

BND = 9
(BND_DU, BND_ABS, BND_PRODUCT, BND_BETA, BND_BETA_PEAK, BND_H, BND_H_PEAK, BND_OVER, BND_FLAG) = range(BND)
STATE_BIT, DECAY_BIT = NS, NS + 5


def build(nc, x, w_in, w_x, w_out, w_r, w_k, w_v, params, a_log, w_dt, b_dt, ident_in, weights_in,
          out, row_scratch):
    import concourse.bass as bass
    from concourse import mybir

    fp32, i32 = mybir.dt.float32, mybir.dt.int32
    ALU = mybir.AluOpType
    ACT = mybir.ActivationFunctionType
    X = mybir.AxisListType.X
    LOGEXP = "natural_log_exp_and_others"

    with ExitStack() as ctx:
        def sb(name, shape, dt=fp32):
            return ctx.enter_context(nc.sbuf_tensor(name, shape, dt))

        def pb(name, shape):
            return ctx.enter_context(nc.psum_tensor(name, shape, fp32))

        def sem(name):
            return ctx.enter_context(nc.semaphore(name))

        win = sb("win", [P, KT, 2 * DI])
        wx = sb("wx", [P, QT, XROWS])
        wout = sb("wout", [P, QT, DM])
        wr = sb("wr", [P, KT, DM])
        wk = sb("wk", [P, KT, DM])
        wv = sb("wv", [P, KT, DM])
        par = sb("par", [P, P_N])
        ident = sb("ident", [P, P])
        bitw = sb("bitw", [P, 3])
        epst = sb("epst", [P, 1])
        a_pos = sb("a_pos", [P, NS])
        a_neg = sb("a_neg", [P, NS])
        a_col = sb("a_col", [NS, 1])
        a_over = sb("a_over", [NS, 1])
        a_top = sb("a_top", [P, 1])
        w_peak = sb("w_peak", [NS, 1])
        b_low = sb("b_low", [NS, 1])
        xin = sb("xin", [P, CH, DM])
        xnT = sb("xnT", [P, KT, LEN])
        xc = sb("xc", [P, QT, TAPS - 1 + LEN])
        acc = sb("acc", [P, QT, LEN])
        rows = xin[0:XROWS, 0:2, :].rearrange("p a b -> p (a b)")
        dtrep = xnT[:, 0, :]
        fst = sb("fst", [P, CH, 6])
        fmv = sb("fmv", [P, CH, 2])
        frs = sb("frs", [P, CH])
        babs = sb("babs", [P, CH, NS])
        beta = sb("beta", [P, CH, NS])
        du_peak = sb("du_peak", [P, CH])
        peak = sb("peak", [NS, 2])
        flag = sb("flag", [P, 3])
        decay_low = xc[0:NS, 0, TAPS - 1:]
        h_bound = xc[0:NS, 1, TAPS - 1:]
        u = sb("u", [P, 2, QT, LEN])
        gate = sb("gate", [P, 2, QT, LEN])
        dt = sb("dt", [P, 2, QT, LEN])
        duT = sb("duT", [P, 2, CH, DI])
        BT = sb("BT", [P, 2, CH, NS])
        word = sb("word", [1, 2], i32)
        decay = sb("decay", [P, 2, QT, LEN])
        bT = sb("bT", [P, 2, CH, DI])
        h = sb("h", [P, H_RING, QT, LEN])
        cring = sb("cring", [P, 2, CG, LEN])
        hmax = sb("hmax", [P, 32])
        hmaxT = sb("hmaxT", [P, 32])
        hq = sb("hq", [P, 4])
        hover = sb("hover", [1, 1], i32)
        hstep = sb("hstep", [P, 1])
        yT = sb("yT", [P, CH, DI])
        x2n = yT[:, 0:2, :].rearrange("p a (b c) -> p (a b) c", c=DM)
        diff = yT[:, 2:4, :]
        kact = yT[:, 2:4, :]
        e = sb("e", [P, QT, LEN])
        xr = e[:, 0:2, :]
        xk = e[:, 2:4, :]
        w_dt_rows = e[0:NS, 0, :]
        b_dt_rows = e[0:NS, 1, :]
        x1 = sb("x1", [P, CH, DM])
        x2T = sb("x2T", [P, KT, 1 + LEN])
        rec = x2T[:, :, 1:1 + LEN]
        recT = rec.rearrange("p a (b c) -> p a b c", c=DM)
        bst = sb("bst", [P, CH, 6])
        bmv = sb("bmv", [P, CH, 2])
        brs = sb("brs", [P, CH])

        yps = [pb(f"yps{c}", [P, DI]) for c in range(CH)]
        bps = [pb(f"bps{i}", [P, LEN]) for i in range(2)]
        fps = pb("fps", [P, 512])
        kps = pb("kps", [P, 512])

        w_loaded = sem("w_loaded")
        zeros_set = sem("zeros_set")
        a_cut = sem("a_cut")
        a_exp = sem("a_exp")
        a_done = sem("a_done")
        x_loaded = sem("x_loaded")
        fagg = sem("fagg")
        fln = sem("fln")
        frstd = sem("frstd")
        xn_ready = sem("xn_ready")
        front_full = sem("front_full")
        front_free = sem("front_free")
        conv_step = sem("conv_step")
        u_ready = sem("u_ready")
        gate_ready = sem("gate_ready")
        rows_stored = sem("rows_stored")
        dtrep_loaded = sem("dtrep_loaded")
        dt_exp = sem("dt_exp")
        dt_capped = sem("dt_capped")
        dt_ln = sem("dt_ln")
        dt_ready = sem("dt_ready")
        du_ready = sem("du_ready")
        low_step = sem("low_step")
        bnd_step = sem("bnd_step")
        c_loaded = [sem(f"c_loaded{i}") for i in range(2)]
        decay_ready = sem("decay_ready")
        bT_act = sem("bT_act")
        bT_dve = sem("bT_dve")
        b_full = sem("b_full")
        h_ready = sem("h_ready")
        p_ready = sem("p_ready")
        p_summed = sem("p_summed")
        yT_act = sem("yT_act")
        yT_dve = sem("yT_dve")
        bagg = sem("bagg")
        bln = sem("bln")
        brstd = sem("brstd")
        yn_ready = sem("yn_ready")
        back_full = sem("back_full")
        back_free = sem("back_free")
        skip_added = sem("skip_added")
        gated = sem("gated")
        xres_loaded = sem("xres_loaded")
        x2n_ready = sem("x2n_ready")
        diff_ready = sem("diff_ready")
        mixed = sem("mixed")
        squared = sem("squared")
        rec_step = sem("rec_step")
        out_ready = sem("out_ready")
        stored = sem("stored")

        def cnt(b, per, k):
            return b * per + (k + 1)

        def front_done(b, name, i=0):
            return cnt(b, NF, FRONT[name, i][0])

        def back_done(b, name, i=0):
            return cnt(b, NBK, BACK[name, i][0])

        def static(v):
            return isinstance(v, int)

        def not_first(v, k=0):
            return not static(v) or v + k > 0

        def slots_of(table, name):
            return {s: i for (nm, i), (_, s) in table.items() if nm == name}

        F = {nm: slots_of(FRONT, nm) for nm, _ in FRONT}
        K = {nm: slots_of(BACK, nm) for nm, _ in BACK}

        def periods(eng, body):
            body(0, 0, True, False, False)
            body(1, 1, True, True, False)
            with eng.Fori(1, SEQS // 2) as i:
                for parity in range(2):
                    body(2 * i + parity, parity, True, True, True)
            body(SEQS, 0, False, True, True)
            body(SEQS + 1, 1, False, False, True)

        def weight_loads():
            return ((win, w_in.rearrange("(k p) m -> p k m", p=P)), (wx, w_x.rearrange("(k p) m -> p k m", p=P)),
                    (wout, w_out.rearrange("(k p) m -> p k m", p=P)), (wr, w_r.rearrange("(k p) m -> p k m", p=P)),
                    (wk, w_k.rearrange("(k p) m -> p k m", p=P)), (wv, w_v.rearrange("(k p) m -> p k m", p=P)),
                    (par, params), (ident, ident_in), (bitw, weights_in),
                    (a_pos, a_log.partition_broadcast(P)), (a_col, a_log.rearrange("(n o) -> n o", o=1)),
                    (w_dt_rows, w_dt.partition_broadcast(NS)), (b_dt_rows, b_dt.partition_broadcast(NS)))

        W_ALL = 16 * 13

        block = ctx.enter_context(nc.Block())

        @block.sync
        def _(sp):
            for t, src in weight_loads():
                dst = t[:, :] if len(t.shape) == 2 else t[:, :, :]
                sp.dma_start(dst, src).then_inc(w_loaded, 16)

            def load_c(b, parity, g):
                r = g % 2
                if g >= 2 or not_first(b):
                    sp.wait_ge(p_ready, cnt(b, 2 * NS, 2 * CG * (g - 1) - 1))
                src = row_scratch[parity, CG * g:CG * (g + 1), :].rearrange("a t -> (a t)")
                sp.dma_start(cring[:, r, :, :].rearrange("p a t -> p (a t)"), src.partition_broadcast(P)) \
                    .then_inc(c_loaded[r], 16)

            def body(p, parity, front, units, back):
                fb, ub = p, p - 1
                for s in range(UNITS):
                    if units and s % (UNITS // NCG) == 0 and s // (UNITS // NCG) + 1 < NCG:
                        load_c(ub, 1 - parity, s // (UNITS // NCG) + 1)
                    if front and s == 38:
                        sp.wait_ge(front_free, front_done(fb, "rows"))
                        sp.dma_start(row_scratch[parity], rows[NS:XROWS, :]).then_inc(rows_stored, 16)
                        sp.wait_ge(rows_stored, 16 * fb + 16)
                        sp.dma_start(dtrep, row_scratch[parity, NS:NS + 1, :].rearrange("a t -> (a t)")
                                     .partition_broadcast(P)).then_inc(dtrep_loaded, 16)
                if front:
                    load_c(fb, parity, 0)

            periods(sp, body)
            sp.wait_ge(rows_stored, 16 * SEQS)

        @block.tensor
        def _(pe):
            pe.wait_ge(w_loaded, W_ALL)

            def turn(dst, src, start=True, stop=True):
                return nc.tensor.matmul(dst, src, ident[0:src.shape[0], 0:src.shape[0]], start=start, stop=stop,
                                        is_transpose=True, skip_group_check=True)

            def unit_input(b, n, q):
                k = QT * n + q
                if n > 1 or (k > 1) or not_first(b):
                    if k >= 2 or not_first(b):
                        pe.wait_ge(h_ready, cnt(b, UNITS, k - 2))
                if q == 0 and n in BT_ON_DVE:
                    pe.wait_ge(bT_dve, cnt(b, len(BT_ON_DVE), BT_ON_DVE.index(n)))
                elif q == 0:
                    pe.wait_ge(bT_act, cnt(b, len(BT_ON_ACT), BT_ON_ACT.index(n)))
                for c in range(CH):
                    last = turn(bps[k % 2][:, c * P:(c + 1) * P], bT[:, n % 2, c, q * P:(q + 1) * P])
                last.then_inc(b_full, 1)

            def unit_sum(b, n, q):
                if q % 2 == 0:
                    pe.wait_ge(p_ready, cnt(b, 2 * NS, 2 * n + q // 2))
                if n == 0 and q == 0 and not_first(b):
                    pe.wait_ge(yT_act, 2 * b)
                    pe.wait_ge(yT_dve, 2 * b)
                for c in range(CH):
                    last = turn(yps[c][:, q * P:(q + 1) * P], h[:, n % H_RING, q, c * P:(c + 1) * P],
                                start=(n == 0 and q == 0), stop=(n == NS - 1))
                last.then_inc(p_summed, 1)

            def front_bank(b, name, i=0):
                k = FRONT[name, i][0]
                if k > 0 or not_first(b):
                    pe.wait_ge(front_free, cnt(b, NF, k - 1))

            def back_bank(b, name, i=0):
                k = BACK[name, i][0]
                if k > 0 or not_first(b):
                    pe.wait_ge(back_free, cnt(b, NBK, k - 1))

            def front_step(b, parity, s, held):
                if s in F["xT"]:
                    k = F["xT"][s]
                    front_bank(b, "xT", k)
                    pe.wait_ge(xn_ready, b + 1)
                    for c in range(CH):
                        last = turn(fps[:, c * P:(c + 1) * P], xin[:, c, k * P:(k + 1) * P])
                    last.then_inc(front_full, 1)
                for name, first in (("xc", 0), ("z", QT)):
                    if s in F[name]:
                        m = F[name][s]
                        front_bank(b, name, m)
                        for k in range(KT):
                            last = nc.tensor.matmul(fps[:, :], win[:, k, (first + m) * P:(first + m + 1) * P],
                                                    xnT[:, k, :], start=(k == 0), stop=(k == KT - 1))
                        last.then_inc(front_full, 1)
                if s in F["rows"]:
                    front_bank(b, "rows")
                    pe.wait_ge(u_ready, b + 1)
                    for k in range(QT):
                        last = nc.tensor.matmul(fps[0:XROWS, :], wx[:, k, :], u[:, parity, k, :],
                                                start=(k == 0), stop=(k == QT - 1))
                    last.then_inc(front_full, 1)
                if s in F["BT"]:
                    if not held:
                        front_bank(b, "BT")
                    for c in range(CH):
                        last = turn(fps[:, c * NS:(c + 1) * NS], rows[0:NS, c * P:(c + 1) * P])
                    last.then_inc(front_full, 1)
                if s in F["duT"]:
                    c = F["duT"][s]
                    front_bank(b, "duT", c)
                    pe.wait_ge(du_ready, b + 1)
                    for q in range(QT):
                        last = turn(fps[:, q * P:(q + 1) * P], acc[:, q, c * P:(c + 1) * P])
                    last.then_inc(front_full, 1)
                if s in F["beta"]:
                    front_bank(b, "beta")
                    pe.wait_ge(bnd_step, cnt(b, BND, BND_BETA))
                    for c in range(CH):
                        last = turn(fps[0:NS, c * P:(c + 1) * P], beta[:, c, :])
                    last.then_inc(front_full, 1)
                if s in F["mask"]:
                    front_bank(b, "mask")
                    pe.wait_ge(bnd_step, cnt(b, BND, BND_FLAG))
                    for k in range(3):
                        last = nc.tensor.matmul(fps[0:1, 0:1], flag[:, k:k + 1], bitw[:, k:k + 1],
                                                start=(k == 0), stop=(k == 2))
                    last.then_inc(front_full, 1)

            def back_step(b, s):
                if s in K["yn"]:
                    q = K["yn"][s]
                    back_bank(b, "yn", q)
                    pe.wait_ge(yn_ready, b + 1)
                    for c in range(CH):
                        last = turn(kps[:, c * P:(c + 1) * P], yT[:, c, q * P:(q + 1) * P])
                    last.then_inc(back_full, 1)
                if s in K["out"]:
                    j = K["out"][s]
                    back_bank(b, "out", j)
                    pe.wait_ge(gated, b + 1)
                    for c in range(2):
                        t = 2 * j + c
                        for k in range(QT):
                            last = nc.tensor.matmul(kps[:, c * DM:(c + 1) * DM], e[:, k, t * P:(t + 1) * P],
                                                    wout[:, k, :], start=(k == 0), stop=(k == QT - 1))
                    last.then_inc(back_full, 1)
                if s in K["x2T"]:
                    k = K["x2T"][s]
                    back_bank(b, "x2T", k)
                    pe.wait_ge(x2n_ready, b + 1)
                    for c in range(CH):
                        last = turn(kps[:, c * P:(c + 1) * P], x2n[:, c, k * P:(k + 1) * P])
                    last.then_inc(back_full, 1)
                if s in K["key"]:
                    m = K["key"][s]
                    back_bank(b, "key", m)
                    pe.wait_ge(mixed, 2 * b + 2)
                    for k in range(KT):
                        last = nc.tensor.matmul(kps[:, :], wk[:, k, m * P:(m + 1) * P], xk[:, k, :],
                                                start=(k == 0), stop=(k == KT - 1))
                    last.then_inc(back_full, 1)
                for name, w, act in (("rec", wr, xr), ("val", wv, kact)):
                    if s in K[name]:
                        j = K[name][s]
                        back_bank(b, name, j)
                        if name == "val":
                            pe.wait_ge(squared, b + 1)
                        for c in range(2):
                            t = 2 * j + c
                            for k in range(KT):
                                last = nc.tensor.matmul(kps[:, c * DM:(c + 1) * DM], act[:, k, t * P:(t + 1) * P],
                                                        w[:, k, :], start=(k == 0), stop=(k == KT - 1))
                        last.then_inc(back_full, 1)

            def body(p, parity, front, units, back):
                for s in range(UNITS):
                    n, q = divmod(s, QT)
                    if front and units and s in F["BT"]:
                        front_bank(p, "BT")
                    if units:
                        unit_input(p - 1, n, q)
                    if front:
                        front_step(p, parity, s, units)
                    if back:
                        back_step(p - 2, s)
                    if n >= SUM_LAG and units:
                        unit_sum(p - 1, n - SUM_LAG, q)
                    elif n < SUM_LAG and back:
                        unit_sum(p - 2, NS - SUM_LAG + n, q)

            periods(pe, body)

        @block.scalar
        def _(act):
            nc.scalar.preload_act_table_set(LOGEXP)
            act.wait_ge(a_cut, 2)
            nc.scalar.activation(a_pos[:, :], a_pos[:, :], ACT.Exp).then_inc(a_exp, 1)
            nc.scalar.activation(a_col[:, :], a_col[:, :], ACT.Exp).then_inc(a_exp, 1)
            act.wait_ge(a_done, 1)

            def unit_terms(b, parity, n, part):
                if part < 2 and n not in BT_ON_DVE:
                    if n == 0 and part == 0:
                        act.wait_ge(front_free, front_done(b, "duT", CH - 1))
                    if part == 0 and (n >= 2 or not_first(b)):
                        act.wait_ge(b_full, cnt(b, UNITS, QT * (n - 1) - 1))
                    for c in (2 * part, 2 * part + 1):
                        last = nc.scalar.activation(bT[:, n % 2, c, :], duT[:, parity, c, :], ACT.Copy,
                                                    scale=BT[:, parity, c, n:n + 1])
                    if part == 1:
                        last.then_inc(bT_act, 1)
                if part == 2:
                    if n == 0:
                        act.wait_ge(dt_ready, b + 1)
                    if n >= 2 or not_first(b):
                        act.wait_ge(h_ready, cnt(b, UNITS, QT * (n - 1) - 1))
                    nc.scalar.activation(decay[:, n % 2, :, :], dt[:, parity, :, :], ACT.Exp,
                                         scale=a_neg[:, n:n + 1]).then_inc(decay_ready, 1)

            def rstd(mv, rs, ln_sem, done_sem, value):
                nc.scalar.activation(rs[:, :], mv[:, :, 1], ACT.Ln, bias=epst[:, 0:1]).then_inc(ln_sem, 1)
                act.wait_ge(ln_sem, value)
                nc.scalar.activation(rs[:, :], rs[:, :], ACT.Exp, scale=-0.5).then_inc(done_sem, 1)

            def front_step(b, parity, s):
                def ready(name, i=0):
                    act.wait_ge(front_full, front_done(b, name, i))
                if s == 3:
                    act.wait_ge(fagg, b + 1)
                    rstd(fmv, frs, fln, frstd, b + 1)
                if s in F["xT"]:
                    k = F["xT"][s]
                    ready("xT", k)
                    if k == 0 and not_first(b):
                        act.wait_ge(dt_exp, b)
                    nc.scalar.activation(xnT[:, k, :], fps[:, :], ACT.Copy).then_inc(front_free, 1)
                if s in F["xc"]:
                    m = F["xc"][s]
                    ready("xc", m)
                    nc.scalar.activation(xc[:, m, TAPS - 1:], fps[:, :], ACT.Copy).then_inc(front_free, 1)
                if s in F["z"]:
                    m = F["z"][s]
                    ready("z", m)
                    if m == 0 and (not_first(b, -1)):
                        act.wait_ge(gated, b - 1)
                    nc.scalar.activation(gate[:, parity, m, :], fps[:, :], ACT.Copy).then_inc(front_free, 1)
                if s in F["rows"]:
                    ready("rows")
                    nc.scalar.activation(rows[:, :], fps[0:XROWS, :], ACT.Copy).then_inc(front_free, 1)
                if s in F["BT"]:
                    ready("BT")
                    nc.scalar.activation(BT[:, parity, :, :], fps[:, 0:CH * NS].rearrange("p (c n) -> p c n", n=NS),
                                         ACT.Copy).then_inc(front_free, 1)
                if s == 43:
                    act.wait_ge(dtrep_loaded, 16 * b + 16)
                    for q in range(QT):
                        last = nc.scalar.activation(dt[:, parity, q, :], dtrep, ACT.Exp,
                                                    scale=par[:, P_WDT + q:P_WDT + q + 1],
                                                    bias=par[:, P_BDT + q:P_BDT + q + 1])
                    last.then_inc(dt_exp, 1)
                if s == 45:
                    act.wait_ge(dt_capped, b + 1)
                    nc.scalar.activation(dt[:, parity, :, :], dt[:, parity, :, :], ACT.Ln, bias=1.0) \
                        .then_inc(dt_ln, 1)
                if s in (47, 48, 49):
                    k = s - 47
                    act.wait_ge(low_step, cnt(b, 4, k))
                    func, scale, bias = ((ACT.Exp, w_peak[:, 0:1], b_low[:, 0:1]), (ACT.Ln, 1.0, 1.0),
                                         (ACT.Exp, a_col[:, 0:1], 0.0))[k]
                    nc.scalar.activation(decay_low, decay_low, func, scale=scale, bias=bias).then_inc(low_step, 1)
                if s in F["duT"]:
                    c = F["duT"][s]
                    ready("duT", c)
                    nc.scalar.activation(duT[:, parity, c, :], fps[:, :], ACT.Copy).then_inc(front_free, 1)

            def back_step(b, s):
                def ready(name, i=0):
                    act.wait_ge(back_full, back_done(b, name, i))
                if s == 8:
                    act.wait_ge(p_summed, UNITS * b + UNITS)
                    for c in range(2):
                        nc.scalar.activation(yT[:, c, :], yps[c][:, :], ACT.Copy).then_inc(yT_act, 1)
                if s == 13:
                    act.wait_ge(bagg, 2 * b + 1)
                    rstd(bmv, brs, bln, brstd, 2 * b + 1)
                if s in K["yn"]:
                    q = K["yn"][s]
                    ready("yn", q)
                    nc.scalar.activation(e[:, q, :], kps[:, :], ACT.Identity, scale=par[:, P_G + q:P_G + q + 1],
                                         bias=par[:, P_B + q:P_B + q + 1]).then_inc(back_free, 1)
                if s == 36:
                    act.wait_ge(bagg, 2 * b + 2)
                    rstd(bmv, brs, bln, brstd, 2 * b + 2)
                if s in K["x2T"]:
                    k = K["x2T"][s]
                    ready("x2T", k)
                    nc.scalar.activation(x2T[:, k, 1:], kps[:, :], ACT.Copy).then_inc(back_free, 1)
                if s in K["key"]:
                    m = K["key"][s]
                    ready("key", m)
                    nc.scalar.activation(kact[:, m, :], kps[:, :], ACT.Relu).then_inc(back_free, 1)
                if 53 <= s < 56:
                    k = s - 53
                    if k == 0:
                        act.wait_ge(back_free, back_done(b, "rec", 1))
                    else:
                        act.wait_ge(rec_step, cnt(b, 3, k - 1))
                    func, scale, bias = ((ACT.Exp, -1.0, 0.0), (ACT.Ln, 1.0, 1.0), (ACT.Exp, -1.0, 0.0))[k]
                    nc.scalar.activation(rec, rec, func, scale=scale, bias=bias).then_inc(rec_step, 1)

            def nonlinear(p, parity):
                if True:
                    act.wait_ge(conv_step, cnt(p, TAPS * QT, TAPS * QT - 1))
                    nc.scalar.activation(u[:, parity, :, :], acc[:, :, :], ACT.Silu).then_inc(u_ready, 1)
                    act.wait_ge(front_free, front_done(p, "z", QT - 1))
                    nc.scalar.activation(gate[:, parity, :, :], gate[:, parity, :, :], ACT.Silu) \
                        .then_inc(gate_ready, 1)
                nc.scalar.preload_act_table_set(LOGEXP)

            def in_chunks(t):
                return t.rearrange("(c t) d -> t c d", t=P)

            def load_x(fb, kb, front, back):
                if front:
                    if not_first(fb):
                        act.wait_ge(front_free, front_done(fb - 1, "BT"))
                        act.wait_ge(rows_stored, 16 * fb)
                    act.dma_start(xin[:, :, :], in_chunks(x[fb])).then_inc(x_loaded, 16)
                if back:
                    if not_first(kb):
                        act.wait_ge(stored, 16 * kb)
                    act.dma_start(x1[:, :, :], in_chunks(x[kb])).then_inc(xres_loaded, 16)

            def body(p, parity, front, units, back):
                load_x(p, p - 2, front, back)
                for s in range(UNITS):
                    n, q = divmod(s, QT)
                    if units and q < 3 and n + 1 < NS:
                        unit_terms(p - 1, 1 - parity, n + 1, q)
                    if front and q < 3 and n + 1 == NS:
                        unit_terms(p, parity, 0, q)
                    if back:
                        back_step(p - 2, s)
                    if front:
                        front_step(p, parity, s)
                    if front and s == 32:
                        nonlinear(p, parity)
                    if back and s == 63:
                        act.wait_ge(out_ready, p - 1)
                        act.dma_start(in_chunks(out[p - 2]), x1[:, :, :]).then_inc(stored, 16)

            periods(act, body)
            act.wait_ge(stored, 16 * SEQS)

        @block.gpsimd
        def _(pool):
            nc.gpsimd.memset(xc[:, :, 0:TAPS - 1], 0.0).then_inc(zeros_set, 1)
            nc.gpsimd.memset(x2T[:, :, 0:1], 0.0).then_inc(zeros_set, 1)
            nc.gpsimd.memset(hmax[:, :], 0.0).then_inc(zeros_set, 1)
            nc.gpsimd.memset(epst[:, :], LN_EPS).then_inc(zeros_set, 1)
            nc.gpsimd.memset(flag[:, 0:2], 0.0).then_inc(zeros_set, 1)
            pool.wait_ge(zeros_set, 5)

            def unit_product(b, n, half):
                if half == 0 and n % CG == 0:
                    g = n // CG
                    pool.wait_ge(c_loaded[g % 2], cnt(b, NCG // 2, g // 2) * 16)
                pool.wait_ge(h_ready, cnt(b, UNITS, QT * n + 2 * half + 1))
                hs = h[:, n % H_RING, 2 * half:2 * half + 2, :]
                cs = cring[:, (n // CG) % 2, n % CG:n % CG + 1, :].broadcast_to([P, 2, LEN])
                nc.gpsimd.tensor_tensor(hs, hs, cs, ALU.mult).then_inc(p_ready, 1)

            def body(p, parity, front, units, back):
                for s in range(UNITS):
                    n, q = divmod(s, QT)
                    if units and q % 2 == 1:
                        unit_product(p - 1, n, q // 2)
                    if back and s == 22:
                        pool.wait_ge(skip_added, p - 1)
                        pool.wait_ge(gate_ready, p - 1)
                        nc.gpsimd.tensor_tensor(e[:, :, :], e[:, :, :], gate[:, parity, :, :], ALU.mult) \
                            .then_inc(gated, 1)
                    if back and s == 42:
                        pool.wait_ge(back_free, back_done(p - 2, "x2T", 1))
                        nc.gpsimd.tensor_tensor(diff, x2T[:, :, 1:], x2T[:, :, 0:LEN], ALU.subtract) \
                            .then_inc(diff_ready, 1)
                    if back and s == 49:
                        pool.wait_ge(back_free, back_done(p - 2, "key", 1))
                        nc.gpsimd.tensor_tensor(kact, kact, kact, ALU.mult).then_inc(squared, 1)
                    if front and s == 47:
                        pool.wait_ge(dt_ready, p + 1)
                        pool.wait_ge(u_ready, p + 1)
                        nc.gpsimd.tensor_tensor(acc[:, :, :], dt[:, parity, :, :], u[:, parity, :, :], ALU.mult) \
                            .then_inc(du_ready, 1)

            periods(pool, body)

        @block.vector
        def _(dve):
            V = nc.vector
            dve.wait_ge(w_loaded, W_ALL)
            dve.wait_ge(zeros_set, 5)
            V.tensor_scalar(a_pos[:, :], a_pos[:, :], 5.0, None, ALU.min).then_inc(a_cut, 1)
            V.tensor_scalar(a_col[:, :], a_col[:, :], 5.0, None, ALU.min).then_inc(a_cut, 1)
            dve.wait_ge(a_exp, 2)
            V.tensor_scalar(a_over[:, :], a_col[:, :], MARGIN * ARG_CLIP / DT_MAX, None, ALU.is_gt)
            V.tensor_reduce(a_top[:, :], a_pos[:, :], X, ALU.max)
            V.tensor_reduce(w_peak[:, :], w_dt_rows, X, ALU.max, apply_absolute_value=True)
            V.tensor_reduce(b_low[:, :], b_dt_rows, X, ALU.min)
            dve.drain()
            V.tensor_scalar(flag[:, 2:3], a_top[:, :], MARGIN * ARG_CLIP / DT_MAX, None, ALU.is_gt)
            V.tensor_scalar(a_col[:, :], a_col[:, :], -1.0, None, ALU.mult)
            V.tensor_scalar(w_peak[:, :], w_peak[:, :], -1.0, None, ALU.mult)
            V.tensor_scalar(b_low[:, :], b_low[:, :], B_LOW_CAP, None, ALU.min)
            V.tensor_scalar(a_neg[:, :], a_pos[:, :], -1.0, None, ALU.mult).then_inc(a_done, 1)
            dve.wait_ge(a_done, 1)

            def scan(n, q):
                return V.tensor_tensor_scan(h[:, n % H_RING, q, :], decay[:, n % 2, q, :],
                                            bps[(QT * n + q) % 2][:, :], 0.0, ALU.mult, ALU.add)

            def clipped_steps(n, q):
                hq_, dq_, bq_ = h[:, n % H_RING, q, :], decay[:, n % 2, q, :], bps[(QT * n + q) % 2]
                V.tensor_scalar(hq_[:, 0:1], bq_[:, 0:1], STATE_CLIP, -STATE_CLIP, ALU.min, ALU.max)
                dve.drain()
                with dve.Fori(1, LEN) as t:
                    V.scalar_tensor_tensor(hstep[:, :], hq_[:, bass.ds(t - 1, 1)], dq_[:, bass.ds(t, 1)],
                                           bq_[:, bass.ds(t, 1)], ALU.mult, ALU.add)
                    dve.drain()
                    V.tensor_scalar(hq_[:, bass.ds(t, 1)], hstep[:, :], STATE_CLIP, -STATE_CLIP, ALU.min, ALU.max)
                    dve.drain()

            def state_over_clip(n, q):
                V.tensor_reduce(hmax[:, 0:1], h[:, n % H_RING, q, :], X, ALU.max, apply_absolute_value=True)
                dve.drain()
                V.transpose(hmaxT[:, :], hmax[:, :])
                dve.drain()
                for k in range(4):
                    V.tensor_reduce(hq[0:1, k:k + 1], hmaxT[32 * k:32 * k + 1, :], X, ALU.max)
                dve.drain()
                V.tensor_reduce(hstep[0:1, :], hq[0:1, :], X, ALU.max)
                dve.drain()
                V.tensor_scalar(hover[:, :], hstep[0:1, :], STATE_CLIP, None, ALU.is_gt)
                dve.drain()
                return dve.value_load(hover[0:1, 0:1], min_val=0, max_val=1)

            def unit_scan(b, n, q, bits):
                k = QT * n + q

                def inputs_ready():
                    if q == 0:
                        dve.wait_ge(decay_ready, cnt(b, NS, n))
                    if n >= H_RING or not_first(b):
                        dve.wait_ge(p_summed, cnt(b, UNITS, k - QT * H_RING))
                    dve.wait_ge(b_full, cnt(b, UNITS, k))

                with dve.If(((bits >> n) & 1) > 0):
                    inputs_ready()
                    bk, dk = bps[k % 2], decay[:, n % 2, q, :]
                    V.tensor_scalar(bk[:, :], bk[:, :], IN_CLIP, -IN_CLIP, ALU.min, ALU.max)
                    with dve.If((bits >> DECAY_BIT) > 0):
                        V.tensor_scalar(dk, dk, DECAY_MIN, None, ALU.max)
                    dve.drain()
                    with dve.If(((bits >> STATE_BIT) & (2 ** (DECAY_BIT - STATE_BIT) - 1)) > 0):
                        scan(n, q)
                        dve.drain()
                        over = state_over_clip(n, q)
                        with dve.If(over > 0):
                            clipped_steps(n, q)
                        dve.sem_inc(h_ready, 1)
                    with dve.Else():
                        scan(n, q).then_inc(h_ready, 1)
                with dve.Else():
                    inputs_ready()
                    scan(n, q).then_inc(h_ready, 1)

            def bT_share(b, parity, n, c):
                if c == 0 and (n >= 2 or not_first(b)):
                    dve.wait_ge(b_full, cnt(b, UNITS, QT * (n - 1) - 1))
                if n == 0 and c == 0:
                    dve.wait_ge(front_free, front_done(b, "duT", CH - 1))
                ins = V.tensor_scalar(bT[:, n % 2, c, :], duT[:, parity, c, :], BT[:, parity, c, n:n + 1], None,
                                      ALU.mult)
                if c == CH - 1:
                    ins.then_inc(bT_dve, 1)

            def stats(st, mv, src, agg_sem):
                for c in range(CH):
                    last = V.bn_stats(st[:, c, :], src[:, c, :])
                dve.drain()
                aggregate(st, mv, agg_sem)

            def aggregate(st, mv, agg_sem):
                for c in range(CH):
                    last = V.bn_aggr(mv[:, c, :], st[:, c, :])
                last.then_inc(agg_sem, 1)

            def normalise(dst, src, mv, rs, done_sem):
                for c in range(CH):
                    last = V.tensor_scalar(dst[:, c, :], src[:, c, :], mv[:, c, 0:1], rs[:, c:c + 1],
                                           ALU.subtract, ALU.mult)
                last.then_inc(done_sem, 1)

            def front_step(b, parity, s):
                if s == 1:
                    dve.wait_ge(x_loaded, 16 * b + 16)
                    if not_first(b):
                        dve.wait_ge(frstd, b)
                    stats(fst, fmv, xin, fagg)
                if s == 4:
                    dve.wait_ge(frstd, b + 1)
                    normalise(xin, xin, fmv, frs, xn_ready)
                if CONV_SLOT <= s < CONV_SLOT + TAPS * QT:
                    tap, q = divmod(s - CONV_SLOT, QT)
                    w = TAPS - 1 - tap
                    if tap == 0:
                        dve.wait_ge(front_free, front_done(b, "xc", q))
                        if not_first(b) and q == 0:
                            dve.wait_ge(front_free, front_done(b - 1, "duT", CH - 1))
                    else:
                        dve.wait_ge(conv_step, cnt(b, TAPS * QT, s - CONV_SLOT - QT))
                    wcol = par[:, P_CW + TAPS * q + w:P_CW + TAPS * q + w + 1]
                    if tap == 0:
                        V.tensor_scalar(acc[:, q, :], xc[:, q, w:w + LEN], wcol, par[:, P_CB + q:P_CB + q + 1],
                                        ALU.mult, ALU.add).then_inc(conv_step, 1)
                    else:
                        V.scalar_tensor_tensor(acc[:, q, :], xc[:, q, w:w + LEN], wcol, acc[:, q, :],
                                               ALU.mult, ALU.add).then_inc(conv_step, 1)
                if s == 44:
                    dve.wait_ge(dt_exp, b + 1)
                    V.tensor_scalar(dt[:, parity, :, :], dt[:, parity, :, :], SOFTPLUS_CAP, None, ALU.min) \
                        .then_inc(dt_capped, 1)
                if s == 46:
                    dve.wait_ge(dt_ln, b + 1)
                    V.tensor_scalar(dt[:, parity, :, :], dt[:, parity, :, :], DT_MIN, DT_MAX, ALU.max, ALU.min) \
                        .then_inc(dt_ready, 1)
                if s == 42:
                    dve.wait_ge(dtrep_loaded, 16 * b + 16)
                    V.scalar_tensor_tensor(decay_low, dtrep[0:NS, :], -1.0, dtrep[0:NS, :], ALU.mult, ALU.max) \
                        .then_inc(low_step, 1)
                if s - 1 in F["duT"]:
                    c = F["duT"][s - 1]
                    dve.wait_ge(front_free, front_done(b, "duT", c))
                    ins = V.tensor_reduce(du_peak[:, c:c + 1], duT[:, parity, c, :], X, ALU.max,
                                          apply_absolute_value=True)
                    if c == CH - 1:
                        ins.then_inc(bnd_step, 1)
                        V.scalar_tensor_tensor(babs[:, :, :], BT[:, parity, :, :], -1.0, BT[:, parity, :, :],
                                               ALU.mult, ALU.max).then_inc(bnd_step, 1)
                        dve.wait_ge(bnd_step, cnt(b, BND, BND_ABS))
                        V.tensor_tensor(beta[:, :, :], babs[:, :, :],
                                        du_peak[:, :].unsqueeze(2).broadcast_to([P, CH, NS]), ALU.mult) \
                            .then_inc(bnd_step, 1)
                        dve.wait_ge(bnd_step, cnt(b, BND, BND_PRODUCT))
                        V.tensor_scalar(beta[:, :, :], beta[:, :, :], IN_CLIP, None, ALU.min).then_inc(bnd_step, 1)
                if s in F["beta"]:
                    dve.wait_ge(front_full, front_done(b, "beta"))
                    V.tensor_reduce(peak[:, 0:1], fps[0:NS, :], X, ALU.max).then_inc(bnd_step, 1)
                if s - 1 in F["beta"]:
                    dve.wait_ge(low_step, 4 * b + 4)
                    V.tensor_tensor_scan(h_bound, decay_low, fps[0:NS, :], 0.0, ALU.mult, ALU.add) \
                        .then_inc(bnd_step, 1)
                    dve.wait_ge(bnd_step, cnt(b, BND, BND_H))
                    V.tensor_reduce(peak[:, 1:2], h_bound, X, ALU.max).then_inc(bnd_step, 1)
                    dve.wait_ge(bnd_step, cnt(b, BND, BND_H_PEAK))
                    V.tensor_scalar(flag[0:NS, 1:2], peak[:, 1:2], MARGIN * STATE_CLIP, None, ALU.is_gt)
                    V.scalar_tensor_tensor(flag[0:NS, 0:1], peak[:, 0:1], MARGIN * IN_CLIP, a_over[:, :],
                                           ALU.is_gt, ALU.max).then_inc(bnd_step, 1)
                    dve.wait_ge(bnd_step, cnt(b, BND, BND_OVER))
                    V.tensor_tensor(flag[0:NS, 0:1], flag[0:NS, 0:1], flag[0:NS, 1:2], ALU.max) \
                        .then_inc(bnd_step, 1)
                    dve.sem_inc(front_free, 1)
                if s - 1 in F["mask"]:
                    dve.wait_ge(front_full, front_done(b, "mask"))
                    V.tensor_copy(word[0:1, parity:parity + 1], fps[0:1, 0:1]).then_inc(front_free, 1)

            def back_step(b, parity, s):
                if s == 8:
                    dve.wait_ge(p_summed, UNITS * b + UNITS)
                    for c in range(2, CH):
                        V.tensor_copy(yT[:, c, :], yps[c][:, :]).then_inc(yT_dve, 1)
                if 9 <= s < 9 + CH:
                    c = s - 9
                    if c == 0:
                        dve.wait_ge(yT_act, 2 * b + 2)
                        dve.wait_ge(yT_dve, 2 * b + 2)
                    V.bn_stats(bst[:, c, :], yT[:, c, :])
                    if c == CH - 1:
                        dve.drain()
                        aggregate(bst, bmv, bagg)
                if s == 14:
                    dve.wait_ge(brstd, 2 * b + 1)
                    normalise(yT, yT, bmv, brs, yn_ready)
                if 18 <= s < 18 + QT:
                    q = s - 18
                    dve.wait_ge(back_free, back_done(b, "yn", q))
                    ins = V.scalar_tensor_tensor(e[:, q, :], u[:, parity, q, :], par[:, P_D + q:P_D + q + 1],
                                                 e[:, q, :], ALU.mult, ALU.add)
                    if q == QT - 1:
                        ins.then_inc(skip_added, 1)
                if s - 1 in K["out"]:
                    j = K["out"][s - 1]
                    dve.wait_ge(back_full, back_done(b, "out", j))
                    dve.wait_ge(xres_loaded, 16 * b + 16)
                    xs = x1[:, 2 * j:2 * j + 2, :]
                    V.tensor_tensor(xs, kps[:, :].rearrange("p (c d) -> p c d", d=DM), xs, ALU.add) \
                        .then_inc(back_free, 1)
                if s == 35:
                    dve.wait_ge(back_free, back_done(b, "out", 1))
                    stats(bst, bmv, x1, bagg)
                if s == 38:
                    dve.wait_ge(brstd, 2 * b + 2)
                    normalise(x2n, x1, bmv, brs, x2n_ready)
                if s in (44, 45):
                    if s == 44:
                        dve.wait_ge(diff_ready, b + 1)
                    dst, col = ((xr, P_MR), (xk, P_MK))[s - 44]
                    for k in range(KT):
                        last = V.scalar_tensor_tensor(dst[:, k, :], diff[:, k, :], par[:, col + k:col + k + 1],
                                                      x2T[:, k, 0:LEN], ALU.mult, ALU.add)
                    last.then_inc(mixed, 1)
                if s in K["rec"]:
                    j = K["rec"][s]
                    dve.wait_ge(back_full, back_done(b, "rec", j))
                    V.tensor_scalar(rec[:, j, :], kps[:, :], R_MIN, None, ALU.max).then_inc(back_free, 1)
                if s in K["val"]:
                    j = K["val"][s]
                    if j == 0:
                        dve.wait_ge(rec_step, 3 * b + 3)
                    dve.wait_ge(back_full, back_done(b, "val", j))
                    V.tensor_tensor(rec[:, j, :], rec[:, j, :], kps[:, :], ALU.mult).then_inc(back_free, 1)
                if s == 61:
                    dve.wait_ge(back_free, back_done(b, "val", 1))
                    x1h = x1[:, :, :].rearrange("p (a c) d -> p a (c d)", a=2)
                    V.tensor_tensor(x1h, rec, x1h, ALU.add).then_inc(out_ready, 1)

            def body(p, parity, front, units, back):
                if units:
                    dve.drain()
                    bits = dve.value_load(word[0:1, 1 - parity:2 - parity], min_val=0,
                                          max_val=2 ** (DECAY_BIT + 1) - 1)
                    if 0 in BT_ON_DVE:
                        for c in range(CH):
                            bT_share(p - 1, 1 - parity, 0, c)
                for s in range(UNITS):
                    n, q = divmod(s, QT)
                    if units:
                        unit_scan(p - 1, n, q, bits)
                        if n + 1 in BT_ON_DVE and q < 2:
                            for c in (2 * q, 2 * q + 1):
                                bT_share(p - 1, 1 - parity, n + 1, c)
                    if back:
                        back_step(p - 2, parity, s)
                    if front:
                        front_step(p, parity, s)

            periods(dve, body)


def kernel(L0_attn_x, L0_attn_W_in, L0_attn_conv_w, L0_attn_conv_b, L0_attn_W_x, L0_attn_W_dt, L0_attn_b_dt,
           L0_attn_A_log, L0_attn_D_param, L0_attn_W_out, L0_attn_ln_g, L0_attn_ln_b, L0_ffn_W_r, L0_ffn_W_k,
           L0_ffn_W_v, L0_ffn_mu_r, L0_ffn_mu_k):
    import numpy as np
    import concourse.bacc as bacc
    from concourse import mybir
    from concourse.bass_utils import run_bass_kernel_spmd

    def cols(v, n):
        return np.ascontiguousarray(np.asarray(v).reshape(n, P).T)

    conv = np.asarray(L0_attn_conv_w).reshape(QT, P, TAPS).transpose(1, 0, 2).reshape(P, QT * TAPS)
    params = np.concatenate([conv] + [cols(v, QT) for v in (L0_attn_conv_b, L0_attn_W_dt, L0_attn_b_dt,
                                                            L0_attn_D_param, L0_attn_ln_g, L0_attn_ln_b)]
                            + [cols(v, KT) for v in (L0_ffn_mu_r, L0_ffn_mu_k)], axis=1)
    w_x = np.asarray(L0_attn_W_x)
    bit_weights = np.zeros((P, 3), np.float32)
    bit_weights[:NS, 0] = 2.0 ** np.arange(NS)
    bit_weights[:NS, 1] = 2.0 ** STATE_BIT
    bit_weights[0, 2] = 2.0 ** DECAY_BIT
    arrays = {
        "x": np.asarray(L0_attn_x), "w_in": np.asarray(L0_attn_W_in).T,
        "w_x": np.concatenate([w_x[1:], w_x[:1]], axis=0).T, "w_out": np.asarray(L0_attn_W_out).T,
        "w_r": np.asarray(L0_ffn_W_r).T, "w_k": np.asarray(L0_ffn_W_k).T, "w_v": np.asarray(L0_ffn_W_v).T,
        "params": params, "a_log": np.asarray(L0_attn_A_log),
        "w_dt": np.asarray(L0_attn_W_dt).reshape(DI), "b_dt": np.asarray(L0_attn_b_dt),
        "ident": np.eye(P, dtype=np.float32), "bit_weights": bit_weights,
    }
    nc = bacc.Bacc("TRN2", target_bir_lowering=False, num_devices=1)
    fp32 = mybir.dt.float32
    ins = {f"{k}_dram": np.ascontiguousarray(v) for k, v in arrays.items()}
    aps = [nc.dram_tensor(k, v.shape, fp32, kind="ExternalInput").ap() for k, v in ins.items()]
    out = nc.dram_tensor("out_dram", (SEQS, LEN, DM), fp32, kind="ExternalOutput").ap()
    scratch = nc.dram_tensor("row_scratch", (2, NS + 1, LEN), fp32, kind="Internal").ap()
    build(nc, *aps, out, scratch)
    return run_bass_kernel_spmd(nc, [ins], core_ids=[0]).results[0]["out_dram"]
```

```python
import math
from contextlib import ExitStack

SEQS, LEN, DM, DI, NS, TAPS = 16, 512, 256, 512, 16, 4
P = 128
QT = DI // P
KT = DM // P
CH = LEN // P
UNITS = NS * QT
XROWS = 2 * NS + 1
LN_EPS = 1e-5
DT_MIN, DT_MAX = 1e-4, 10.0
IN_CLIP, STATE_CLIP, ARG_CLIP = 10.0, 100.0, 20.0
DECAY_MIN = math.exp(-ARG_CLIP)
MARGIN = 0.995
B_LOW_CAP = 9.9
SOFTPLUS_CAP = 1e9
R_MIN = -43.0
CG = 2
NCG = NS // CG
H_RING = 4
SUM_LAG = 7

AT = dict(x_stats=3, x_rstd=4, x_norm=5, conv=12, silu=28, rows_out=36, dt_exp=40, low_abs=40, dt_cap=41,
          dt_ln=43, dt_clip=44, low=(46, 48, 50), du=(45, 46, 47, 48), y_copy=SUM_LAG, y_stats=8, y_rstd=11,
          y_norm=13, x1_stats=32, x1_rstd=33, x1_norm=34, diff=(37, 38), mix=(40, 41), square=(44, 46),
          sigmoid=(52, 53, 54), add=59, store=61)

P_CW, P_CB, P_WDT, P_BDT, P_D, P_G, P_B = 0, 16, 20, 24, 28, 32, 36
P_MR, P_MK, P_N = 40, 42, 44


def bank_uses(**slots):
    uses = sorted((slot, name, i) for name, at in slots.items() for i, slot in enumerate(at))
    return {(name, i): (k, slot) for k, (slot, name, i) in enumerate(uses)}


FRONT = bank_uses(xT=(7, 8), xc=(9, 13, 17, 21), rows=(35,), BT=(39,), z=(37, 41, 50, 59),
                  duT=(51, 53, 55, 57), beta=(60,), mask=(62,))
BACK = bank_uses(yn=(15, 16, 18, 19), out=(25, 27, 29, 31), x2T=(36, 37), key=(43, 45), rec=(47, 49),
                 val=(56, 58))
NF, NBK = len(FRONT), len(BACK)

BND = 8
(BND_DU, BND_ABS, BND_PRODUCT, BND_BETA, BND_BETA_PEAK, BND_H_PEAK, BND_OVER, BND_FLAG) = range(BND)
STATE_BIT, DECAY_BIT = NS, NS + 5


def build(nc, x, w_in, w_x, w_out, w_r, w_k, w_v, params, a_log, w_dt, b_dt, ident_in, weights_in,
          out, row_scratch):
    import concourse.bass as bass
    from concourse import mybir

    fp32, i32 = mybir.dt.float32, mybir.dt.int32
    ALU = mybir.AluOpType
    ACT = mybir.ActivationFunctionType
    X = mybir.AxisListType.X
    LOGEXP = "natural_log_exp_and_others"

    with ExitStack() as ctx:
        def sb(name, shape, dt=fp32):
            return ctx.enter_context(nc.sbuf_tensor(name, shape, dt))

        def pb(name, shape):
            return ctx.enter_context(nc.psum_tensor(name, shape, fp32))

        def sem(name):
            return ctx.enter_context(nc.semaphore(name))

        win = sb("win", [P, KT, 2 * DI])
        wx = sb("wx", [P, QT, XROWS])
        wout = sb("wout", [P, QT, DM])
        wr = sb("wr", [P, KT, DM])
        wk = sb("wk", [P, KT, DM])
        wv = sb("wv", [P, KT, DM])
        par = sb("par", [P, P_N])
        ident = sb("ident", [P, P])
        bitw = sb("bitw", [P, 3])
        epst = sb("epst", [P, 1])
        a_pos = sb("a_pos", [P, NS])
        a_neg = sb("a_neg", [P, NS])
        a_col = sb("a_col", [NS, 1])
        a_over = sb("a_over", [NS, 1])
        a_top = sb("a_top", [P, 1])
        w_peak = sb("w_peak", [NS, 1])
        b_low = sb("b_low", [NS, 1])
        xin = sb("xin", [P, CH, DM])
        xnT = sb("xnT", [P, KT, LEN])
        xc = sb("xc", [P, QT, TAPS - 1 + LEN])
        acc = sb("acc", [P, QT, LEN])
        rows = xin[0:XROWS, 0:2, :].rearrange("p a b -> p (a b)")
        dtrep = acc[:, 0, :]
        fst = sb("fst", [P, CH, 6])
        fmv = sb("fmv", [P, CH, 2])
        frs = sb("frs", [P, CH])
        babs = sb("babs", [P, CH, NS])
        beta = sb("beta", [P, CH, NS])
        du_peak = sb("du_peak", [P, CH])
        peak = sb("peak", [NS, 2])
        flag = sb("flag", [P, 3])
        decay_low = xc[0:NS, 0, TAPS - 1:]
        h_bound = xc[0:NS, 1, TAPS - 1:]
        u = sb("u", [P, 2, QT, LEN])
        gate = sb("gate", [P, 2, QT, LEN])
        dt = sb("dt", [P, 2, QT, LEN])
        duT = sb("duT", [P, 2, CH, DI])
        BT = sb("BT", [P, 2, CH, NS])
        word = sb("word", [1, 2], i32)
        decay = sb("decay", [P, 2, QT, LEN])
        bT = sb("bT", [P, 2, CH, DI])
        h = sb("h", [P, H_RING, QT, LEN])
        cring = sb("cring", [P, 2, CG, LEN])
        hmax = sb("hmax", [P, 32])
        hmaxT = sb("hmaxT", [P, 32])
        hq = sb("hq", [P, 4])
        hover = sb("hover", [1, 1], i32)
        hstep = sb("hstep", [P, 1])
        yT = sb("yT", [P, CH, DI])
        x2n = yT[:, 0:2, :].rearrange("p a (b c) -> p (a b) c", c=DM)
        diff = yT[:, 2:4, :]
        kact = yT[:, 2:4, :]
        e = sb("e", [P, QT, LEN])
        xr = e[:, 0:2, :]
        xk = e[:, 2:4, :]
        w_dt_rows = e[0:NS, 0, :]
        b_dt_rows = e[0:NS, 1, :]
        x1 = sb("x1", [P, CH, DM])
        x2T = sb("x2T", [P, KT, 1 + LEN])
        rec = x2T[:, :, 1:1 + LEN]
        recT = rec.rearrange("p a (b c) -> p a b c", c=DM)
        bst = sb("bst", [P, CH, 6])
        bmv = sb("bmv", [P, CH, 2])
        brs = sb("brs", [P, CH])

        yps = [pb(f"yps{c}", [P, DI]) for c in range(CH)]
        bps = [pb(f"bps{i}", [P, LEN]) for i in range(2)]
        fps = pb("fps", [P, 512])
        kps = pb("kps", [P, 512])

        small_loaded = sem("small_loaded")
        win_loaded = sem("win_loaded")
        w_loaded = sem("w_loaded")
        zeros_set = sem("zeros_set")
        a_cut = sem("a_cut")
        a_exp = sem("a_exp")
        a_done = sem("a_done")
        x_loaded = sem("x_loaded")
        fagg = sem("fagg")
        fln = sem("fln")
        frstd = sem("frstd")
        xn_ready = sem("xn_ready")
        front_full = sem("front_full")
        front_free = sem("front_free")
        conv_step = sem("conv_step")
        u_ready = sem("u_ready")
        gate_ready = sem("gate_ready")
        rows_stored = sem("rows_stored")
        dtrep_loaded = sem("dtrep_loaded")
        dt_exp = sem("dt_exp")
        dt_capped = sem("dt_capped")
        dt_ln = sem("dt_ln")
        dt_ready = sem("dt_ready")
        du_ready = sem("du_ready")
        low_step = sem("low_step")
        bnd_step = sem("bnd_step")
        c_loaded = [sem(f"c_loaded{i}") for i in range(2)]
        decay_ready = sem("decay_ready")
        bT_ready = sem("bT_ready")
        b_full = sem("b_full")
        h_ready = sem("h_ready")
        p_ready = sem("p_ready")
        p_summed = sem("p_summed")
        yT_act = sem("yT_act")
        yT_dve = sem("yT_dve")
        bagg = sem("bagg")
        bln = sem("bln")
        brstd = sem("brstd")
        yn_ready = sem("yn_ready")
        back_full = sem("back_full")
        back_free = sem("back_free")
        skip_added = sem("skip_added")
        gated = sem("gated")
        xres_loaded = sem("xres_loaded")
        x2n_ready = sem("x2n_ready")
        diff_ready = sem("diff_ready")
        mixed = sem("mixed")
        squared = sem("squared")
        rec_step = sem("rec_step")
        out_ready = sem("out_ready")
        stored = sem("stored")

        def cnt(b, per, k):
            return b * per + (k + 1)

        def front_done(b, name, i=0):
            return cnt(b, NF, FRONT[name, i][0])

        def back_done(b, name, i=0):
            return cnt(b, NBK, BACK[name, i][0])

        def static(v):
            return isinstance(v, int)

        def not_first(v, k=0):
            return not static(v) or v + k > 0

        def slots_of(table, name):
            return {s: i for (nm, i), (_, s) in table.items() if nm == name}

        F = {nm: slots_of(FRONT, nm) for nm, _ in FRONT}
        K = {nm: slots_of(BACK, nm) for nm, _ in BACK}

        def periods(eng, body):
            body(0, 0, True, False, False)
            body(1, 1, True, True, False)
            with eng.Fori(1, SEQS // 2) as i:
                for parity in range(2):
                    body(2 * i + parity, parity, True, True, True)
            body(SEQS, 0, False, True, True)
            body(SEQS + 1, 1, False, False, True)

        def small_loads():
            return ((ident, ident_in), (a_pos, a_log.partition_broadcast(P)),
                    (a_col, a_log.rearrange("(n o) -> n o", o=1)), (w_dt_rows, w_dt.partition_broadcast(NS)),
                    (b_dt_rows, b_dt.partition_broadcast(NS)), (par, params), (bitw, weights_in))

        def weight_loads():
            return ((win, w_in.rearrange("(k p) m -> p k m", p=P)), (wx, w_x.rearrange("(k p) m -> p k m", p=P)),
                    (wout, w_out.rearrange("(k p) m -> p k m", p=P)), (wr, w_r.rearrange("(k p) m -> p k m", p=P)),
                    (wk, w_k.rearrange("(k p) m -> p k m", p=P)), (wv, w_v.rearrange("(k p) m -> p k m", p=P)))

        SMALL_ALL = 16 * 7
        W_ALL = 16 * 5

        block = ctx.enter_context(nc.Block())

        @block.sync
        def _(sp):
            for t, src in small_loads():
                sp.dma_start(t[:, :] if len(t.shape) == 2 else t[:, :, :], src).then_inc(small_loaded, 16)
            for t, src in weight_loads():
                sp.dma_start(t[:, :, :], src).then_inc(win_loaded if t is win else w_loaded, 16)

            def load_c(b, parity, g):
                r = g % 2
                if g >= 2 or not_first(b):
                    sp.wait_ge(p_ready, cnt(b, 2 * NS, 2 * CG * (g - 1) - 1))
                src = row_scratch[parity, CG * g:CG * (g + 1), :].rearrange("a t -> (a t)")
                sp.dma_start(cring[:, r, :, :].rearrange("p a t -> p (a t)"), src.partition_broadcast(P)) \
                    .then_inc(c_loaded[r], 16)

            def body(p, parity, front, units, back):
                fb, ub = p, p - 1
                for s in range(UNITS):
                    if units and s % (UNITS // NCG) == 0 and s // (UNITS // NCG) + 1 < NCG:
                        load_c(ub, 1 - parity, s // (UNITS // NCG) + 1)
                    if front and s == AT["rows_out"]:
                        sp.wait_ge(front_free, front_done(fb, "rows"))
                        sp.dma_start(row_scratch[parity], rows[NS:XROWS, :]).then_inc(rows_stored, 16)
                        sp.wait_ge(rows_stored, 16 * fb + 16)
                        sp.dma_start(dtrep, row_scratch[parity, NS:NS + 1, :].rearrange("a t -> (a t)")
                                     .partition_broadcast(P)).then_inc(dtrep_loaded, 16)
                if front:
                    load_c(fb, parity, 0)

            periods(sp, body)
            sp.wait_ge(rows_stored, 16 * SEQS)

        @block.tensor
        def _(pe):
            pe.wait_ge(small_loaded, SMALL_ALL)

            def turn(dst, src, start=True, stop=True):
                return nc.tensor.matmul(dst, src, ident[0:src.shape[0], 0:src.shape[0]], start=start, stop=stop,
                                        is_transpose=True, skip_group_check=True)

            def unit_input(b, n, q):
                k = QT * n + q
                if k >= 2 or not_first(b):
                    pe.wait_ge(h_ready, cnt(b, UNITS, k - 2))
                if q == 0:
                    pe.wait_ge(bT_ready, cnt(b, NS, n))
                for c in range(CH):
                    last = turn(bps[k % 2][:, c * P:(c + 1) * P], bT[:, n % 2, c, q * P:(q + 1) * P])
                last.then_inc(b_full, 1)

            def unit_sum(b, n, q):
                if q % 2 == 0:
                    pe.wait_ge(p_ready, cnt(b, 2 * NS, 2 * n + q // 2))
                if n == 0 and q == 0 and not_first(b):
                    pe.wait_ge(yT_act, 2 * b)
                    pe.wait_ge(yT_dve, 2 * b)
                for c in range(CH):
                    last = turn(yps[c][:, q * P:(q + 1) * P], h[:, n % H_RING, q, c * P:(c + 1) * P],
                                start=(n == 0 and q == 0), stop=(n == NS - 1))
                last.then_inc(p_summed, 1)

            def front_bank(b, name, i=0):
                k = FRONT[name, i][0]
                if k > 0 or not_first(b):
                    pe.wait_ge(front_free, cnt(b, NF, k - 1))

            def back_bank(b, name, i=0):
                k = BACK[name, i][0]
                if k > 0 or not_first(b):
                    pe.wait_ge(back_free, cnt(b, NBK, k - 1))

            def front_step(b, parity, s, held):
                if s in F["xT"]:
                    k = F["xT"][s]
                    front_bank(b, "xT", k)
                    pe.wait_ge(xn_ready, b + 1)
                    for c in range(CH):
                        last = turn(fps[:, c * P:(c + 1) * P], xin[:, c, k * P:(k + 1) * P])
                    last.then_inc(front_full, 1)
                for name, first in (("xc", 0), ("z", QT)):
                    if s in F[name]:
                        m = F[name][s]
                        front_bank(b, name, m)
                        if name == "xc" and m == 0 and not not_first(b):
                            pe.wait_ge(win_loaded, 16)
                        for k in range(KT):
                            last = nc.tensor.matmul(fps[:, :], win[:, k, (first + m) * P:(first + m + 1) * P],
                                                    xnT[:, k, :], start=(k == 0), stop=(k == KT - 1))
                        last.then_inc(front_full, 1)
                if s + 2 in F["rows"]:
                    if not not_first(b):
                        pe.wait_ge(w_loaded, W_ALL)
                    front_bank(b, "rows")
                    pe.wait_ge(u_ready, b + 1)
                if s + 2 in F["rows"] or s in F["rows"]:
                    first = 0 if s + 2 in F["rows"] else QT // 2
                    for k in range(first, first + QT // 2):
                        last = nc.tensor.matmul(fps[0:XROWS, :], wx[:, k, :], u[:, parity, k, :],
                                                start=(k == 0), stop=(k == QT - 1))
                    if s in F["rows"]:
                        last.then_inc(front_full, 1)
                if s in F["BT"]:
                    if not held:
                        front_bank(b, "BT")
                    for c in range(CH):
                        last = turn(fps[:, c * NS:(c + 1) * NS], rows[0:NS, c * P:(c + 1) * P])
                    last.then_inc(front_full, 1)
                if s in F["duT"]:
                    c = F["duT"][s]
                    front_bank(b, "duT", c)
                    pe.wait_ge(du_ready, QT * b + QT)
                    for q in range(QT):
                        last = turn(fps[:, q * P:(q + 1) * P], acc[:, q, c * P:(c + 1) * P])
                    last.then_inc(front_full, 1)
                if s in F["beta"]:
                    front_bank(b, "beta")
                    pe.wait_ge(bnd_step, cnt(b, BND, BND_BETA))
                    for c in range(CH):
                        last = turn(fps[0:NS, c * P:(c + 1) * P], beta[:, c, :])
                    last.then_inc(front_full, 1)
                if s in F["mask"]:
                    front_bank(b, "mask")
                    pe.wait_ge(bnd_step, cnt(b, BND, BND_FLAG))
                    for k in range(3):
                        last = nc.tensor.matmul(fps[0:1, 0:1], flag[:, k:k + 1], bitw[:, k:k + 1],
                                                start=(k == 0), stop=(k == 2))
                    last.then_inc(front_full, 1)

            def back_step(b, s):
                if s in K["yn"]:
                    q = K["yn"][s]
                    back_bank(b, "yn", q)
                    pe.wait_ge(yn_ready, b + 1)
                    for c in range(CH):
                        last = turn(kps[:, c * P:(c + 1) * P], yT[:, c, q * P:(q + 1) * P])
                    last.then_inc(back_full, 1)
                if s in K["out"]:
                    j = K["out"][s]
                    back_bank(b, "out", j)
                    pe.wait_ge(gated, QT * b + QT)
                    for k in range(QT):
                        last = nc.tensor.matmul(kps[:, 0:DM], e[:, k, j * P:(j + 1) * P], wout[:, k, :],
                                                start=(k == 0), stop=(k == QT - 1))
                    last.then_inc(back_full, 1)
                if s in K["x2T"]:
                    k = K["x2T"][s]
                    back_bank(b, "x2T", k)
                    pe.wait_ge(x2n_ready, b + 1)
                    for c in range(CH):
                        last = turn(kps[:, c * P:(c + 1) * P], x2n[:, c, k * P:(k + 1) * P])
                    last.then_inc(back_full, 1)
                if s in K["key"]:
                    m = K["key"][s]
                    back_bank(b, "key", m)
                    pe.wait_ge(mixed, 2 * b + 2)
                    for k in range(KT):
                        last = nc.tensor.matmul(kps[:, :], wk[:, k, m * P:(m + 1) * P], xk[:, k, :],
                                                start=(k == 0), stop=(k == KT - 1))
                    last.then_inc(back_full, 1)
                for name, w, act in (("rec", wr, xr), ("val", wv, kact)):
                    if s in K[name]:
                        j = K[name][s]
                        back_bank(b, name, j)
                        if name == "val":
                            pe.wait_ge(squared, KT * b + KT)
                        for c in range(2):
                            t = 2 * j + c
                            for k in range(KT):
                                last = nc.tensor.matmul(kps[:, c * DM:(c + 1) * DM], act[:, k, t * P:(t + 1) * P],
                                                        w[:, k, :], start=(k == 0), stop=(k == KT - 1))
                        last.then_inc(back_full, 1)

            def body(p, parity, front, units, back):
                for s in range(UNITS):
                    n, q = divmod(s, QT)
                    if front and units and s in F["BT"]:
                        front_bank(p, "BT")
                    if units:
                        unit_input(p - 1, n, q)
                    if s < SUM_LAG and back:
                        unit_sum(p - 2, *divmod(UNITS - SUM_LAG + s, QT))
                    if s >= SUM_LAG + 2 and units:
                        for k in ((0, 1, 2) if s == SUM_LAG + 2 else (s - SUM_LAG,)):
                            unit_sum(p - 1, *divmod(k, QT))
                    if front:
                        front_step(p, parity, s, units)
                    if back:
                        back_step(p - 2, s)

            periods(pe, body)

        @block.scalar
        def _(act):
            def in_chunks(t):
                return t.rearrange("(c t) d -> t c d", t=P)

            act.dma_start(xin[:, :, :], in_chunks(x[0])).then_inc(x_loaded, 16)
            nc.scalar.preload_act_table_set(LOGEXP)
            act.wait_ge(a_cut, 2)
            nc.scalar.activation(a_pos[:, :], a_pos[:, :], ACT.Exp).then_inc(a_exp, 1)
            nc.scalar.activation(a_col[:, :], a_col[:, :], ACT.Exp).then_inc(a_exp, 1)
            act.wait_ge(a_done, 1)

            def unit_terms(b, parity, n, part):
                if part < 2:
                    if n == 0 and part == 0:
                        act.wait_ge(front_free, front_done(b, "duT", CH - 1))
                    if part == 0 and (n >= 2 or not_first(b)):
                        act.wait_ge(b_full, cnt(b, UNITS, QT * (n - 1) - 1))
                    for c in (2 * part, 2 * part + 1):
                        last = nc.scalar.activation(bT[:, n % 2, c, :], duT[:, parity, c, :], ACT.Copy,
                                                    scale=BT[:, parity, c, n:n + 1])
                    if part == 1:
                        last.then_inc(bT_ready, 1)
                if part == 2:
                    if n == 0:
                        act.wait_ge(dt_ready, b + 1)
                    if n >= 2 or not_first(b):
                        act.wait_ge(h_ready, cnt(b, UNITS, QT * (n - 1) - 1))
                    nc.scalar.activation(decay[:, n % 2, :, :], dt[:, parity, :, :], ACT.Exp,
                                         scale=a_neg[:, n:n + 1]).then_inc(decay_ready, 1)

            def rstd(mv, rs, ln_sem, done_sem, value):
                nc.scalar.activation(rs[:, :], mv[:, :, 1], ACT.Ln, bias=epst[:, 0:1]).then_inc(ln_sem, 1)
                act.wait_ge(ln_sem, value)
                nc.scalar.activation(rs[:, :], rs[:, :], ACT.Exp, scale=-0.5).then_inc(done_sem, 1)

            def front_step(b, parity, s):
                def ready(name, i=0):
                    act.wait_ge(front_full, front_done(b, name, i))
                if s == AT["x_rstd"]:
                    act.wait_ge(fagg, b + 1)
                    rstd(fmv, frs, fln, frstd, b + 1)
                if s in F["xT"]:
                    k = F["xT"][s]
                    ready("xT", k)
                    nc.scalar.activation(xnT[:, k, :], fps[:, :], ACT.Copy).then_inc(front_free, 1)
                if s in F["xc"]:
                    m = F["xc"][s]
                    ready("xc", m)
                    nc.scalar.activation(xc[:, m, TAPS - 1:], fps[:, :], ACT.Copy).then_inc(front_free, 1)
                if s in F["z"]:
                    m = F["z"][s]
                    ready("z", m)
                    if m == 0 and (not_first(b, -1)):
                        act.wait_ge(gated, QT * (b - 1))
                    nc.scalar.activation(gate[:, parity, m, :], fps[:, :], ACT.Copy).then_inc(front_free, 1)
                if s in F["rows"]:
                    ready("rows")
                    nc.scalar.activation(rows[:, :], fps[0:XROWS, :], ACT.Copy).then_inc(front_free, 1)
                if s in F["BT"]:
                    ready("BT")
                    nc.scalar.activation(BT[:, parity, :, :], fps[:, 0:CH * NS].rearrange("p (c n) -> p c n", n=NS),
                                         ACT.Copy).then_inc(front_free, 1)
                if s == AT["dt_exp"]:
                    act.wait_ge(dtrep_loaded, 16 * b + 16)
                    for q in range(QT):
                        last = nc.scalar.activation(dt[:, parity, q, :], dtrep, ACT.Exp,
                                                    scale=par[:, P_WDT + q:P_WDT + q + 1],
                                                    bias=par[:, P_BDT + q:P_BDT + q + 1])
                    last.then_inc(dt_exp, 1)
                if s == AT["dt_ln"]:
                    act.wait_ge(dt_capped, b + 1)
                    nc.scalar.activation(dt[:, parity, :, :], dt[:, parity, :, :], ACT.Ln, bias=1.0) \
                        .then_inc(dt_ln, 1)
                if s in AT["low"]:
                    k = AT["low"].index(s)
                    act.wait_ge(low_step, cnt(b, 4, k))
                    func, scale, bias = ((ACT.Exp, w_peak[:, 0:1], b_low[:, 0:1]), (ACT.Ln, 1.0, 1.0),
                                         (ACT.Exp, a_col[:, 0:1], 0.0))[k]
                    nc.scalar.activation(decay_low, decay_low, func, scale=scale, bias=bias).then_inc(low_step, 1)
                if s in F["duT"]:
                    c = F["duT"][s]
                    ready("duT", c)
                    nc.scalar.activation(duT[:, parity, c, :], fps[:, :], ACT.Copy).then_inc(front_free, 1)

            def back_step(b, s):
                def ready(name, i=0):
                    act.wait_ge(back_full, back_done(b, name, i))
                if s == AT["y_copy"]:
                    act.wait_ge(p_summed, UNITS * b + UNITS)
                    for c in range(2):
                        nc.scalar.activation(yT[:, c, :], yps[c][:, :], ACT.Copy).then_inc(yT_act, 1)
                if s == AT["y_rstd"]:
                    act.wait_ge(bagg, 2 * b + 1)
                    rstd(bmv, brs, bln, brstd, 2 * b + 1)
                if s in K["yn"]:
                    q = K["yn"][s]
                    ready("yn", q)
                    nc.scalar.activation(e[:, q, :], kps[:, :], ACT.Identity, scale=par[:, P_G + q:P_G + q + 1],
                                         bias=par[:, P_B + q:P_B + q + 1]).then_inc(back_free, 1)
                if s == AT["x1_rstd"]:
                    act.wait_ge(bagg, 2 * b + 2)
                    rstd(bmv, brs, bln, brstd, 2 * b + 2)
                if s in K["x2T"]:
                    k = K["x2T"][s]
                    ready("x2T", k)
                    nc.scalar.activation(x2T[:, k, 1:], kps[:, :], ACT.Copy).then_inc(back_free, 1)
                if s in K["key"]:
                    m = K["key"][s]
                    ready("key", m)
                    nc.scalar.activation(kact[:, m, :], kps[:, :], ACT.Relu).then_inc(back_free, 1)
                if s in AT["sigmoid"]:
                    k = AT["sigmoid"].index(s)
                    if k == 0:
                        act.wait_ge(back_free, back_done(b, "rec", 1))
                    else:
                        act.wait_ge(rec_step, cnt(b, 3, k - 1))
                    func, scale, bias = ((ACT.Exp, -1.0, 0.0), (ACT.Ln, 1.0, 1.0), (ACT.Exp, -1.0, 0.0))[k]
                    nc.scalar.activation(rec, rec, func, scale=scale, bias=bias).then_inc(rec_step, 1)

            def nonlinear(p, parity, front, units):
                if front:
                    act.wait_ge(conv_step, cnt(p, TAPS * QT, TAPS * QT - 1))
                    nc.scalar.activation(u[:, parity, :, :], acc[:, :, :], ACT.Silu).then_inc(u_ready, 1)
                if units:
                    act.wait_ge(front_free, front_done(p - 1, "z", QT - 1))
                    nc.scalar.activation(gate[:, 1 - parity, :, :], gate[:, 1 - parity, :, :], ACT.Silu) \
                        .then_inc(gate_ready, 1)
                nc.scalar.preload_act_table_set(LOGEXP)

            def load_x(fb, kb, front, back):
                if front and not_first(fb):
                    act.wait_ge(front_free, front_done(fb - 1, "BT"))
                    act.wait_ge(rows_stored, 16 * fb)
                    act.dma_start(xin[:, :, :], in_chunks(x[fb])).then_inc(x_loaded, 16)
                if back:
                    if not_first(kb):
                        act.wait_ge(stored, 16 * kb)
                    act.dma_start(x1[:, :, :], in_chunks(x[kb])).then_inc(xres_loaded, 16)

            def body(p, parity, front, units, back):
                load_x(p, p - 2, front, back)
                for s in range(UNITS):
                    n, q = divmod(s, QT)
                    if units and q < 3 and n + 1 < NS:
                        unit_terms(p - 1, 1 - parity, n + 1, q)
                    if front and q < 3 and n + 1 == NS:
                        unit_terms(p, parity, 0, q)
                    if back:
                        back_step(p - 2, s)
                    if front:
                        front_step(p, parity, s)
                    if (front or units) and s == AT["silu"]:
                        nonlinear(p, parity, front, units)
                    if back and s == AT["store"]:
                        act.wait_ge(out_ready, p - 1)
                        act.dma_start(in_chunks(out[p - 2]), x1[:, :, :]).then_inc(stored, 16)

            periods(act, body)
            act.wait_ge(stored, 16 * SEQS)

        @block.gpsimd
        def _(pool):
            nc.gpsimd.memset(xc[:, :, 0:TAPS - 1], 0.0).then_inc(zeros_set, 1)
            nc.gpsimd.memset(x2T[:, :, 0:1], 0.0).then_inc(zeros_set, 1)
            nc.gpsimd.memset(hmax[:, :], 0.0).then_inc(zeros_set, 1)
            nc.gpsimd.memset(epst[:, :], LN_EPS).then_inc(zeros_set, 1)
            nc.gpsimd.memset(flag[:, 0:2], 0.0).then_inc(zeros_set, 1)
            pool.wait_ge(zeros_set, 5)

            def unit_product(b, n, half):
                if half == 0 and n % CG == 0:
                    g = n // CG
                    pool.wait_ge(c_loaded[g % 2], cnt(b, NCG // 2, g // 2) * 16)
                pool.wait_ge(h_ready, cnt(b, UNITS, QT * n + 2 * half + 1))
                hs = h[:, n % H_RING, 2 * half:2 * half + 2, :]
                cs = cring[:, (n // CG) % 2, n % CG:n % CG + 1, :].broadcast_to([P, 2, LEN])
                nc.gpsimd.tensor_tensor(hs, hs, cs, ALU.mult).then_inc(p_ready, 1)

            def body(p, parity, front, units, back):
                for s in range(UNITS):
                    n, q = divmod(s, QT)
                    if units and q % 2 == 1:
                        unit_product(p - 1, n, q // 2)
                    if back and s - 2 in K["yn"]:
                        t = K["yn"][s - 2]
                        pool.wait_ge(skip_added, cnt(p - 2, QT, t))
                        if t == 0:
                            pool.wait_ge(gate_ready, p - 1)
                        nc.gpsimd.tensor_tensor(e[:, t, :], e[:, t, :], gate[:, parity, t, :], ALU.mult) \
                            .then_inc(gated, 1)
                    if back and s in AT["diff"]:
                        k = AT["diff"].index(s)
                        pool.wait_ge(back_free, back_done(p - 2, "x2T", k))
                        nc.gpsimd.tensor_tensor(diff[:, k, :], x2T[:, k, 1:], x2T[:, k, 0:LEN], ALU.subtract) \
                            .then_inc(diff_ready, 1)
                    if back and s in AT["square"]:
                        k = AT["square"].index(s)
                        pool.wait_ge(back_free, back_done(p - 2, "key", k))
                        nc.gpsimd.tensor_tensor(kact[:, k, :], kact[:, k, :], kact[:, k, :], ALU.mult) \
                            .then_inc(squared, 1)
                    if front and s in AT["du"]:
                        t = AT["du"].index(s)
                        if t == 0:
                            pool.wait_ge(dt_ready, p + 1)
                            pool.wait_ge(u_ready, p + 1)
                            pool.wait_ge(low_step, 4 * p + 1)
                        nc.gpsimd.tensor_tensor(acc[:, t, :], dt[:, parity, t, :], u[:, parity, t, :], ALU.mult) \
                            .then_inc(du_ready, 1)

            periods(pool, body)

        @block.vector
        def _(dve):
            V = nc.vector
            dve.wait_ge(small_loaded, SMALL_ALL)
            dve.wait_ge(zeros_set, 5)
            V.tensor_scalar(a_pos[:, :], a_pos[:, :], 5.0, None, ALU.min).then_inc(a_cut, 1)
            V.tensor_scalar(a_col[:, :], a_col[:, :], 5.0, None, ALU.min).then_inc(a_cut, 1)
            dve.wait_ge(a_exp, 2)
            V.tensor_scalar(a_over[:, :], a_col[:, :], MARGIN * ARG_CLIP / DT_MAX, None, ALU.is_gt)
            V.tensor_reduce(a_top[:, :], a_pos[:, :], X, ALU.max)
            V.tensor_reduce(w_peak[:, :], w_dt_rows, X, ALU.max, apply_absolute_value=True)
            V.tensor_reduce(b_low[:, :], b_dt_rows, X, ALU.min)
            dve.drain()
            V.tensor_scalar(flag[:, 2:3], a_top[:, :], MARGIN * ARG_CLIP / DT_MAX, None, ALU.is_gt)
            V.tensor_scalar(a_col[:, :], a_col[:, :], -1.0, None, ALU.mult)
            V.tensor_scalar(w_peak[:, :], w_peak[:, :], -1.0, None, ALU.mult)
            V.tensor_scalar(b_low[:, :], b_low[:, :], B_LOW_CAP, None, ALU.min)
            V.tensor_scalar(a_neg[:, :], a_pos[:, :], -1.0, None, ALU.mult).then_inc(a_done, 1)
            dve.wait_ge(a_done, 1)

            def scan(n, q):
                return V.tensor_tensor_scan(h[:, n % H_RING, q, :], decay[:, n % 2, q, :],
                                            bps[(QT * n + q) % 2][:, :], 0.0, ALU.mult, ALU.add)

            def clipped_steps(n, q):
                hq_, dq_, bq_ = h[:, n % H_RING, q, :], decay[:, n % 2, q, :], bps[(QT * n + q) % 2]
                V.tensor_scalar(hq_[:, 0:1], bq_[:, 0:1], STATE_CLIP, -STATE_CLIP, ALU.min, ALU.max)
                dve.drain()
                with dve.Fori(1, LEN) as t:
                    V.scalar_tensor_tensor(hstep[:, :], hq_[:, bass.ds(t - 1, 1)], dq_[:, bass.ds(t, 1)],
                                           bq_[:, bass.ds(t, 1)], ALU.mult, ALU.add)
                    dve.drain()
                    V.tensor_scalar(hq_[:, bass.ds(t, 1)], hstep[:, :], STATE_CLIP, -STATE_CLIP, ALU.min, ALU.max)
                    dve.drain()

            def state_over_clip(n, q):
                V.tensor_reduce(hmax[:, 0:1], h[:, n % H_RING, q, :], X, ALU.max, apply_absolute_value=True)
                dve.drain()
                V.transpose(hmaxT[:, :], hmax[:, :])
                dve.drain()
                for k in range(4):
                    V.tensor_reduce(hq[0:1, k:k + 1], hmaxT[32 * k:32 * k + 1, :], X, ALU.max)
                dve.drain()
                V.tensor_reduce(hstep[0:1, :], hq[0:1, :], X, ALU.max)
                dve.drain()
                V.tensor_scalar(hover[:, :], hstep[0:1, :], STATE_CLIP, None, ALU.is_gt)
                dve.drain()
                return dve.value_load(hover[0:1, 0:1], min_val=0, max_val=1)

            def unit_scan(b, n, q, bits):
                k = QT * n + q

                def inputs_ready():
                    if q == 0:
                        dve.wait_ge(decay_ready, cnt(b, NS, n))
                    if n >= H_RING or not_first(b):
                        dve.wait_ge(p_summed, cnt(b, UNITS, k - QT * H_RING))
                    dve.wait_ge(b_full, cnt(b, UNITS, k))

                with dve.If(((bits >> n) & 1) > 0):
                    inputs_ready()
                    bk, dk = bps[k % 2], decay[:, n % 2, q, :]
                    V.tensor_scalar(bk[:, :], bk[:, :], IN_CLIP, -IN_CLIP, ALU.min, ALU.max)
                    with dve.If((bits >> DECAY_BIT) > 0):
                        V.tensor_scalar(dk, dk, DECAY_MIN, None, ALU.max)
                    dve.drain()
                    with dve.If(((bits >> STATE_BIT) & (2 ** (DECAY_BIT - STATE_BIT) - 1)) > 0):
                        scan(n, q)
                        dve.drain()
                        over = state_over_clip(n, q)
                        with dve.If(over > 0):
                            clipped_steps(n, q)
                        dve.sem_inc(h_ready, 1)
                    with dve.Else():
                        scan(n, q).then_inc(h_ready, 1)
                with dve.Else():
                    inputs_ready()
                    scan(n, q).then_inc(h_ready, 1)

            def stats(st, mv, src, agg_sem):
                for c in range(CH):
                    last = V.bn_stats(st[:, c, :], src[:, c, :])
                dve.drain()
                aggregate(st, mv, agg_sem)

            def aggregate(st, mv, agg_sem):
                for c in range(CH):
                    last = V.bn_aggr(mv[:, c, :], st[:, c, :])
                last.then_inc(agg_sem, 1)

            def normalise(dst, src, mv, rs, done_sem):
                for c in range(CH):
                    last = V.tensor_scalar(dst[:, c, :], src[:, c, :], mv[:, c, 0:1], rs[:, c:c + 1],
                                           ALU.subtract, ALU.mult)
                last.then_inc(done_sem, 1)

            def front_step(b, parity, s):
                if s == AT["x_stats"]:
                    dve.wait_ge(x_loaded, 16 * b + 16)
                    if not_first(b):
                        dve.wait_ge(frstd, b)
                    stats(fst, fmv, xin, fagg)
                if s == AT["x_norm"]:
                    dve.wait_ge(frstd, b + 1)
                    normalise(xin, xin, fmv, frs, xn_ready)
                if AT["conv"] <= s < AT["conv"] + TAPS * QT:
                    q, tap = divmod(s - AT["conv"], TAPS)
                    w = TAPS - 1 - tap
                    if tap == 0:
                        dve.wait_ge(front_free, front_done(b, "xc", q))
                        if not_first(b) and q == 0:
                            dve.wait_ge(front_free, front_done(b - 1, "duT", CH - 1))
                    else:
                        dve.wait_ge(conv_step, cnt(b, TAPS * QT, s - AT["conv"] - 1))
                    wcol = par[:, P_CW + TAPS * q + w:P_CW + TAPS * q + w + 1]
                    if tap == 0:
                        V.tensor_scalar(acc[:, q, :], xc[:, q, w:w + LEN], wcol, par[:, P_CB + q:P_CB + q + 1],
                                        ALU.mult, ALU.add).then_inc(conv_step, 1)
                    else:
                        V.scalar_tensor_tensor(acc[:, q, :], xc[:, q, w:w + LEN], wcol, acc[:, q, :],
                                               ALU.mult, ALU.add).then_inc(conv_step, 1)
                if s == AT["dt_cap"]:
                    dve.wait_ge(dt_exp, b + 1)
                    V.tensor_scalar(dt[:, parity, :, :], dt[:, parity, :, :], SOFTPLUS_CAP, None, ALU.min) \
                        .then_inc(dt_capped, 1)
                if s == AT["dt_clip"]:
                    dve.wait_ge(dt_ln, b + 1)
                    V.tensor_scalar(dt[:, parity, :, :], dt[:, parity, :, :], DT_MIN, DT_MAX, ALU.max, ALU.min) \
                        .then_inc(dt_ready, 1)
                if s == AT["low_abs"]:
                    dve.wait_ge(dtrep_loaded, 16 * b + 16)
                    V.scalar_tensor_tensor(decay_low, dtrep[0:NS, :], -1.0, dtrep[0:NS, :], ALU.mult, ALU.max) \
                        .then_inc(low_step, 1)
                if s - 1 in F["duT"]:
                    c = F["duT"][s - 1]
                    dve.wait_ge(front_free, front_done(b, "duT", c))
                    ins = V.tensor_reduce(du_peak[:, c:c + 1], duT[:, parity, c, :], X, ALU.max,
                                          apply_absolute_value=True)
                    if c == CH - 1:
                        ins.then_inc(bnd_step, 1)
                        V.scalar_tensor_tensor(babs[:, :, :], BT[:, parity, :, :], -1.0, BT[:, parity, :, :],
                                               ALU.mult, ALU.max).then_inc(bnd_step, 1)
                        dve.wait_ge(bnd_step, cnt(b, BND, BND_ABS))
                        V.tensor_tensor(beta[:, :, :], babs[:, :, :],
                                        du_peak[:, :].unsqueeze(2).broadcast_to([P, CH, NS]), ALU.mult) \
                            .then_inc(bnd_step, 1)
                        dve.wait_ge(bnd_step, cnt(b, BND, BND_PRODUCT))
                        V.tensor_scalar(beta[:, :, :], beta[:, :, :], IN_CLIP, None, ALU.min).then_inc(bnd_step, 1)
                if s in F["beta"]:
                    dve.wait_ge(front_full, front_done(b, "beta"))
                    V.tensor_reduce(peak[:, 0:1], fps[0:NS, :], X, ALU.max).then_inc(bnd_step, 1)
                if s - 1 in F["beta"]:
                    dve.wait_ge(low_step, 4 * b + 4)
                    V.tensor_tensor_scan(h_bound, decay_low, fps[0:NS, :], 0.0, ALU.mult, ALU.add) \
                        .then_inc(front_free, 1)
                    dve.wait_ge(front_free, front_done(b, "beta"))
                    V.tensor_reduce(peak[:, 1:2], h_bound, X, ALU.max).then_inc(bnd_step, 1)
                    dve.wait_ge(bnd_step, cnt(b, BND, BND_H_PEAK))
                    V.tensor_scalar(flag[0:NS, 1:2], peak[:, 1:2], MARGIN * STATE_CLIP, None, ALU.is_gt)
                    V.scalar_tensor_tensor(flag[0:NS, 0:1], peak[:, 0:1], MARGIN * IN_CLIP, a_over[:, :],
                                           ALU.is_gt, ALU.max).then_inc(bnd_step, 1)
                    dve.wait_ge(bnd_step, cnt(b, BND, BND_OVER))
                    V.tensor_tensor(flag[0:NS, 0:1], flag[0:NS, 0:1], flag[0:NS, 1:2], ALU.max) \
                        .then_inc(bnd_step, 1)
                if s - 1 in F["mask"]:
                    dve.wait_ge(front_full, front_done(b, "mask"))
                    V.tensor_copy(word[0:1, parity:parity + 1], fps[0:1, 0:1]).then_inc(front_free, 1)

            def back_step(b, parity, s):
                if s == AT["y_copy"]:
                    dve.wait_ge(p_summed, UNITS * b + UNITS)
                    for c in range(2, CH):
                        V.tensor_copy(yT[:, c, :], yps[c][:, :]).then_inc(yT_dve, 1)
                if AT["y_stats"] <= s < AT["y_stats"] + CH:
                    c = s - AT["y_stats"]
                    if c == 0:
                        dve.wait_ge(yT_act, 2 * b + 2)
                        dve.wait_ge(yT_dve, 2 * b + 2)
                    V.bn_stats(bst[:, c, :], yT[:, c, :])
                    if c == CH - 1:
                        dve.drain()
                        aggregate(bst, bmv, bagg)
                if s == AT["y_norm"]:
                    dve.wait_ge(brstd, 2 * b + 1)
                    normalise(yT, yT, bmv, brs, yn_ready)
                if s - 1 in K["yn"]:
                    q = K["yn"][s - 1]
                    dve.wait_ge(back_free, back_done(b, "yn", q))
                    ins = V.scalar_tensor_tensor(e[:, q, :], u[:, parity, q, :], par[:, P_D + q:P_D + q + 1],
                                                 e[:, q, :], ALU.mult, ALU.add)
                    ins.then_inc(skip_added, 1)
                if s - 1 in K["out"]:
                    j = K["out"][s - 1]
                    dve.wait_ge(back_full, back_done(b, "out", j))
                    dve.wait_ge(xres_loaded, 16 * b + 16)
                    V.tensor_tensor(x1[:, j, :], kps[:, 0:DM], x1[:, j, :], ALU.add).then_inc(back_free, 1)
                if s == AT["x1_stats"]:
                    dve.wait_ge(back_free, back_done(b, "out", CH - 1))
                    stats(bst, bmv, x1, bagg)
                if s == AT["x1_norm"]:
                    dve.wait_ge(brstd, 2 * b + 2)
                    normalise(x2n, x1, bmv, brs, x2n_ready)
                if s in AT["mix"]:
                    if s == AT["mix"][0]:
                        dve.wait_ge(diff_ready, KT * b + KT)
                    dst, col = ((xr, P_MR), (xk, P_MK))[AT["mix"].index(s)]
                    for k in range(KT):
                        last = V.scalar_tensor_tensor(dst[:, k, :], diff[:, k, :], par[:, col + k:col + k + 1],
                                                      x2T[:, k, 0:LEN], ALU.mult, ALU.add)
                    last.then_inc(mixed, 1)
                if s in K["rec"]:
                    j = K["rec"][s]
                    dve.wait_ge(back_full, back_done(b, "rec", j))
                    V.tensor_scalar(rec[:, j, :], kps[:, :], R_MIN, None, ALU.max).then_inc(back_free, 1)
                if s in K["val"]:
                    j = K["val"][s]
                    if j == 0:
                        dve.wait_ge(rec_step, 3 * b + 3)
                    dve.wait_ge(back_full, back_done(b, "val", j))
                    V.tensor_tensor(rec[:, j, :], rec[:, j, :], kps[:, :], ALU.mult).then_inc(back_free, 1)
                if s == AT["add"]:
                    dve.wait_ge(back_free, back_done(b, "val", 1))
                    x1h = x1[:, :, :].rearrange("p (a c) d -> p a (c d)", a=2)
                    V.tensor_tensor(x1h, rec, x1h, ALU.add).then_inc(out_ready, 1)

            def body(p, parity, front, units, back):
                if units:
                    dve.drain()
                    bits = dve.value_load(word[0:1, 1 - parity:2 - parity], min_val=0,
                                          max_val=2 ** (DECAY_BIT + 1) - 1)
                for s in range(UNITS):
                    n, q = divmod(s, QT)
                    if units:
                        unit_scan(p - 1, n, q, bits)
                    if back:
                        back_step(p - 2, parity, s)
                    if front:
                        front_step(p, parity, s)

            periods(dve, body)


def kernel(L0_attn_x, L0_attn_W_in, L0_attn_conv_w, L0_attn_conv_b, L0_attn_W_x, L0_attn_W_dt, L0_attn_b_dt,
           L0_attn_A_log, L0_attn_D_param, L0_attn_W_out, L0_attn_ln_g, L0_attn_ln_b, L0_ffn_W_r, L0_ffn_W_k,
           L0_ffn_W_v, L0_ffn_mu_r, L0_ffn_mu_k):
    import numpy as np
    import concourse.bacc as bacc
    from concourse import mybir
    from concourse.bass_utils import run_bass_kernel_spmd

    def cols(v, n):
        return np.ascontiguousarray(np.asarray(v).reshape(n, P).T)

    conv = np.asarray(L0_attn_conv_w).reshape(QT, P, TAPS).transpose(1, 0, 2).reshape(P, QT * TAPS)
    params = np.concatenate([conv] + [cols(v, QT) for v in (L0_attn_conv_b, L0_attn_W_dt, L0_attn_b_dt,
                                                            L0_attn_D_param, L0_attn_ln_g, L0_attn_ln_b)]
                            + [cols(v, KT) for v in (L0_ffn_mu_r, L0_ffn_mu_k)], axis=1)
    w_x = np.asarray(L0_attn_W_x)
    bit_weights = np.zeros((P, 3), np.float32)
    bit_weights[:NS, 0] = 2.0 ** np.arange(NS)
    bit_weights[:NS, 1] = 2.0 ** STATE_BIT
    bit_weights[0, 2] = 2.0 ** DECAY_BIT
    arrays = {
        "x": np.asarray(L0_attn_x), "w_in": np.asarray(L0_attn_W_in).T,
        "w_x": np.concatenate([w_x[1:], w_x[:1]], axis=0).T, "w_out": np.asarray(L0_attn_W_out).T,
        "w_r": np.asarray(L0_ffn_W_r).T, "w_k": np.asarray(L0_ffn_W_k).T, "w_v": np.asarray(L0_ffn_W_v).T,
        "params": params, "a_log": np.asarray(L0_attn_A_log),
        "w_dt": np.asarray(L0_attn_W_dt).reshape(DI), "b_dt": np.asarray(L0_attn_b_dt),
        "ident": np.eye(P, dtype=np.float32), "bit_weights": bit_weights,
    }
    nc = bacc.Bacc("TRN2", target_bir_lowering=False, num_devices=1)
    fp32 = mybir.dt.float32
    ins = {f"{k}_dram": np.ascontiguousarray(v) for k, v in arrays.items()}
    aps = [nc.dram_tensor(k, v.shape, fp32, kind="ExternalInput").ap() for k, v in ins.items()]
    out = nc.dram_tensor("out_dram", (SEQS, LEN, DM), fp32, kind="ExternalOutput").ap()
    scratch = nc.dram_tensor("row_scratch", (2, NS + 1, LEN), fp32, kind="Internal").ap()
    build(nc, *aps, out, scratch)
    return run_bass_kernel_spmd(nc, [ins], core_ids=[0]).results[0]["out_dram"]
```
